# Optimizing a Trainium2 kernel written in Bass

```python
import numpy as np
import jax
import jax.numpy as jnp

def _softmax(x, axis=-1):
    return jax.nn.softmax(x, axis=axis)

def _gelu(x):
    return jax.nn.gelu(x, approximate=True)

def _silu(x):
    return jax.nn.silu(x)

def _sigmoid(x):
    return jax.nn.sigmoid(x)

def _layernorm(x, axis=-1, eps=1e-05):
    m = jnp.mean(x, axis=axis, keepdims=True)
    v = jnp.var(x, axis=axis, keepdims=True)
    return (x - m) / jnp.sqrt(v + eps)

def _scatter_add(tgt, idx, src, axis=0):
    return tgt.at[idx].add(src)

def _segment_sum(src, seg, n):
    return jax.ops.segment_sum(src, seg, n)
kernel_name = 'mk_seq_postln_d1_jaxref_r4_8d1ddb'

def setup_inputs(seed: int=0):
    np.random.seed(seed)
    _w = jnp.asarray

    def _L0_attn_setup():
        import jax, jax.numpy as jnp
        import numpy as np
        import math
        D = 512
        H = 16
        KV = 4
        DH = D // H
        REP = H // KV
        LAMBDA_INIT = 0.8 - 0.6 * math.exp(-0.3 * 0)
        ROPE_BASE = 10000.0
        EPS = 1e-05

        def _rope(x, cos, sin):
            x1, x2 = (x[..., ::2], x[..., 1::2])
            c = cos[None, None]
            s = sin[None, None]
            o1 = x1 * c - x2 * s
            o2 = x1 * s + x2 * c
            return jnp.stack([o1, o2], axis=-1).reshape(x.shape)

        def _forward(x, Wq, Wk, Wv, Wo, lambda_q1, lambda_k1, lambda_q2, lambda_k2, gn_w, gn_b):
            B, T, _ = x.shape
            q = (x @ Wq).reshape(B, T, H, 2 * DH).transpose(0, 2, 1, 3)
            k = (x @ Wk).reshape(B, T, KV, 2 * DH).transpose(0, 2, 1, 3)
            v = (x @ Wv).reshape(B, T, KV, 2 * DH).transpose(0, 2, 1, 3)
            q1, q2 = (q[..., :DH], q[..., DH:])
            k1, k2 = (k[..., :DH], k[..., DH:])
            inv = 1.0 / ROPE_BASE ** (jnp.arange(0, DH, 2, dtype=jnp.float32) / DH)
            freqs = jnp.arange(T, dtype=jnp.float32)[:, None] * inv[None, :]
            cos, sin = (jnp.cos(freqs), jnp.sin(freqs))
            q1, q2 = (_rope(q1, cos, sin), _rope(q2, cos, sin))
            k1, k2 = (_rope(k1, cos, sin), _rope(k2, cos, sin))
            k1 = jnp.repeat(k1, REP, axis=1)
            k2 = jnp.repeat(k2, REP, axis=1)
            v = jnp.repeat(v, REP, axis=1)
            mask = jnp.triu(jnp.full((T, T), -jnp.inf, dtype=x.dtype), k=1)[None, None]
            scale = 1.0 / math.sqrt(DH)
            s1 = jnp.einsum('bhtd,bhsd->bhts', q1, k1) * scale + mask
            s2 = jnp.einsum('bhtd,bhsd->bhts', q2, k2) * scale + mask
            a1 = jax.nn.softmax(s1, axis=-1)
            a2 = jax.nn.softmax(s2, axis=-1)
            lam = jnp.exp(jnp.sum(lambda_q1 * lambda_k1)) - jnp.exp(jnp.sum(lambda_q2 * lambda_k2)) + LAMBDA_INIT
            diff = a1 - lam * a2
            out = jnp.einsum('bhts,bhsd->bhtd', diff, v)
            out = out.transpose(0, 2, 1, 3)
            mean = jnp.mean(out, axis=(1, 3), keepdims=True)
            var = jnp.var(out, axis=(1, 3), keepdims=True)
            out = (out - mean) * jax.lax.rsqrt(var + EPS)
            out = out * gn_w.reshape(1, 1, H, 2 * DH) + gn_b.reshape(1, 1, H, 2 * DH)
            out = out.reshape(B, T, 2 * H * DH) * (1.0 - LAMBDA_INIT)
            return out @ Wo
        key = jax.random.key(seed)
        ks = jax.random.split(key, 12)
        B, T = (1, 512)
        s = 0.02
        return {'x': jax.random.normal(ks[0], (B, T, D), jnp.float32), 'Wq': jax.random.normal(ks[1], (D, 2 * H * DH), jnp.float32) * s, 'Wk': jax.random.normal(ks[2], (D, 2 * KV * DH), jnp.float32) * s, 'Wv': jax.random.normal(ks[3], (D, 2 * KV * DH), jnp.float32) * s, 'Wo': jax.random.normal(ks[4], (2 * H * DH, D), jnp.float32) * s, 'lambda_q1': jax.random.normal(ks[5], (DH,), jnp.float32) * 0.1, 'lambda_k1': jax.random.normal(ks[6], (DH,), jnp.float32) * 0.1, 'lambda_q2': jax.random.normal(ks[7], (DH,), jnp.float32) * 0.1, 'lambda_k2': jax.random.normal(ks[8], (DH,), jnp.float32) * 0.1, 'gn_w': jnp.ones((2 * H * DH,), jnp.float32), 'gn_b': jnp.zeros((2 * H * DH,), jnp.float32)}
    _L0_attn_in = _L0_attn_setup()

    def _L0_ffn_setup():
        import jax, jax.numpy as jnp
        import numpy as np
        D_MODEL = 512
        D_EXPERT = 2048
        EPS = 1e-08

        def ternary_quant(w):
            scale = jnp.mean(jnp.abs(w)) + EPS
            q = jnp.clip(jnp.round(w / scale), -1.0, 1.0) * scale
            return w + jax.lax.stop_gradient(q - w)
        key = jax.random.key(seed)
        k_x, k_up, k_gate, k_down = jax.random.split(key, 4)
        std_in = 1.0 / np.sqrt(D_MODEL)
        std_exp = 1.0 / np.sqrt(D_EXPERT)
        return {'x': jax.random.normal(k_x, (4, 512, D_MODEL), dtype=jnp.float32), 'W_up': jax.random.normal(k_up, (D_EXPERT, D_MODEL), dtype=jnp.float32) * std_in, 'W_gate': jax.random.normal(k_gate, (D_EXPERT, D_MODEL), dtype=jnp.float32) * std_in, 'W_down': jax.random.normal(k_down, (D_MODEL, D_EXPERT), dtype=jnp.float32) * std_exp}
    _L0_ffn_in = _L0_ffn_setup()
    _d = {'L0_attn_x': _L0_attn_in['x'], 'L0_attn_Wq': _L0_attn_in['Wq'], 'L0_attn_Wk': _L0_attn_in['Wk'], 'L0_attn_Wv': _L0_attn_in['Wv'], 'L0_attn_Wo': _L0_attn_in['Wo'], 'L0_attn_lambda_q1': _L0_attn_in['lambda_q1'], 'L0_attn_lambda_k1': _L0_attn_in['lambda_k1'], 'L0_attn_lambda_q2': _L0_attn_in['lambda_q2'], 'L0_attn_lambda_k2': _L0_attn_in['lambda_k2'], 'L0_attn_gn_w': _L0_attn_in['gn_w'], 'L0_attn_gn_b': _L0_attn_in['gn_b'], 'L0_ffn_W_up': _L0_ffn_in['W_up'], 'L0_ffn_W_gate': _L0_ffn_in['W_gate'], 'L0_ffn_W_down': _L0_ffn_in['W_down']}
    _x0 = _d['L0_attn_x']
    _d['L0_attn_x'] = jax.random.normal(jax.random.fold_in(jax.random.key(seed), 1), (4, 1024, 512), dtype=_x0.dtype)
    del _x0
    return _d

def reference(L0_attn_x, L0_attn_Wq, L0_attn_Wk, L0_attn_Wv, L0_attn_Wo, L0_attn_lambda_q1, L0_attn_lambda_k1, L0_attn_lambda_q2, L0_attn_lambda_k2, L0_attn_gn_w, L0_attn_gn_b, L0_ffn_W_up, L0_ffn_W_gate, L0_ffn_W_down):

    def _L0_attn_ref(x, Wq, Wk, Wv, Wo, lambda_q1, lambda_k1, lambda_q2, lambda_k2, gn_w, gn_b):
        import jax, jax.numpy as jnp
        import numpy as np
        import math
        D = 512
        H = 16
        KV = 4
        DH = D // H
        REP = H // KV
        LAMBDA_INIT = 0.8 - 0.6 * math.exp(-0.3 * 0)
        ROPE_BASE = 10000.0
        EPS = 1e-05

        def _rope(x, cos, sin):
            x1, x2 = (x[..., ::2], x[..., 1::2])
            c = cos[None, None]
            s = sin[None, None]
            o1 = x1 * c - x2 * s
            o2 = x1 * s + x2 * c
            return jnp.stack([o1, o2], axis=-1).reshape(x.shape)

        def _forward(x, Wq, Wk, Wv, Wo, lambda_q1, lambda_k1, lambda_q2, lambda_k2, gn_w, gn_b):
            B, T, _ = x.shape
            q = (x @ Wq).reshape(B, T, H, 2 * DH).transpose(0, 2, 1, 3)
            k = (x @ Wk).reshape(B, T, KV, 2 * DH).transpose(0, 2, 1, 3)
            v = (x @ Wv).reshape(B, T, KV, 2 * DH).transpose(0, 2, 1, 3)
            q1, q2 = (q[..., :DH], q[..., DH:])
            k1, k2 = (k[..., :DH], k[..., DH:])
            inv = 1.0 / ROPE_BASE ** (jnp.arange(0, DH, 2, dtype=jnp.float32) / DH)
            freqs = jnp.arange(T, dtype=jnp.float32)[:, None] * inv[None, :]
            cos, sin = (jnp.cos(freqs), jnp.sin(freqs))
            q1, q2 = (_rope(q1, cos, sin), _rope(q2, cos, sin))
            k1, k2 = (_rope(k1, cos, sin), _rope(k2, cos, sin))
            k1 = jnp.repeat(k1, REP, axis=1)
            k2 = jnp.repeat(k2, REP, axis=1)
            v = jnp.repeat(v, REP, axis=1)
            mask = jnp.triu(jnp.full((T, T), -jnp.inf, dtype=x.dtype), k=1)[None, None]
            scale = 1.0 / math.sqrt(DH)
            s1 = jnp.einsum('bhtd,bhsd->bhts', q1, k1) * scale + mask
            s2 = jnp.einsum('bhtd,bhsd->bhts', q2, k2) * scale + mask
            a1 = jax.nn.softmax(s1, axis=-1)
            a2 = jax.nn.softmax(s2, axis=-1)
            lam = jnp.exp(jnp.sum(lambda_q1 * lambda_k1)) - jnp.exp(jnp.sum(lambda_q2 * lambda_k2)) + LAMBDA_INIT
            diff = a1 - lam * a2
            out = jnp.einsum('bhts,bhsd->bhtd', diff, v)
            out = out.transpose(0, 2, 1, 3)
            mean = jnp.mean(out, axis=(1, 3), keepdims=True)
            var = jnp.var(out, axis=(1, 3), keepdims=True)
            out = (out - mean) * jax.lax.rsqrt(var + EPS)
            out = out * gn_w.reshape(1, 1, H, 2 * DH) + gn_b.reshape(1, 1, H, 2 * DH)
            out = out.reshape(B, T, 2 * H * DH) * (1.0 - LAMBDA_INIT)
            return out @ Wo
        return _forward(x, Wq, Wk, Wv, Wo, lambda_q1, lambda_k1, lambda_q2, lambda_k2, gn_w, gn_b)

    def _L0_ffn_ref(x, W_up, W_gate, W_down):
        import jax, jax.numpy as jnp
        import numpy as np
        D_MODEL = 512
        D_EXPERT = 2048
        EPS = 1e-08

        def ternary_quant(w):
            scale = jnp.mean(jnp.abs(w)) + EPS
            q = jnp.clip(jnp.round(w / scale), -1.0, 1.0) * scale
            return w + jax.lax.stop_gradient(q - w)
        wu = ternary_quant(W_up)
        wg = ternary_quant(W_gate)
        wd = ternary_quant(W_down)
        up = jnp.einsum('bsd,ed->bse', x, wu)
        gate = jnp.einsum('bsd,ed->bse', x, wg)
        hidden = jax.nn.silu(up) * gate
        return jnp.einsum('bse,de->bsd', hidden, wd)
    x = L0_attn_x
    x = _layernorm(x + _L0_attn_ref(x, L0_attn_Wq, L0_attn_Wk, L0_attn_Wv, L0_attn_Wo, L0_attn_lambda_q1, L0_attn_lambda_k1, L0_attn_lambda_q2, L0_attn_lambda_k2, L0_attn_gn_w, L0_attn_gn_b), axis=-1)
    x = _layernorm(x + _L0_ffn_ref(x, L0_ffn_W_up, L0_ffn_W_gate, L0_ffn_W_down), axis=-1)
    return x

_drawn_inputs = setup_inputs


def setup_inputs(seed=0):
    import zlib

    import numpy as np

    out = dict(_drawn_inputs(seed))
    spreads = {'L0_attn_gn_w': (1.0, 0.2), 'L0_attn_gn_b': (0.0, 0.1)}
    factors = {'L0_attn_lambda_q1': 6.016,
     'L0_attn_lambda_k1': 8.0,
     'L0_attn_lambda_q2': 25.311,
     'L0_attn_lambda_k2': 200.0}
    for name, (base, spread) in spreads.items():
        noise = np.random.default_rng([zlib.crc32(name.encode()), seed]).standard_normal(out[name].shape)
        drawn = base * np.exp(spread * noise) if base else spread * noise
        out[name] = jnp.asarray(drawn.astype(out[name].dtype))
    for name, factor in factors.items():
        out[name] = (out[name] * factor).astype(out[name].dtype)
    return out
```

```python
import math
from contextlib import ExitStack

import numpy as np
import concourse.bass as bass
from concourse import mybir

F32, F32R, F16, BF16 = mybir.dt.float32, mybir.dt.float32r, mybir.dt.float16, mybir.dt.bfloat16
F8, I32 = mybir.dt.float8e4, mybir.dt.int32
ACT = mybir.ActivationFunctionType
ALU = mybir.AluOpType
AX = mybir.AxisListType

B, T, D = 4, 1024, 512
H, KV, DH = 16, 4, 32
E = 2048
P = 128
NT = T // P
DC = D // P
EB = E // P
QC = H * 2 * DH
KC = KV * 2 * DH
QKV = QC + 2 * KC
BANK = 512
NH = NT * H
QUADS = NH // 4
LAMBDA_INIT = 0.8 - 0.6 * math.exp(-0.3 * 0)
LN_EPS = 1e-5
TERNARY_EPS = 1e-8
NEG = -3.0e38
HI_BITS = -4096
XS = 1024.0
HS = 8.0


def head_of(i):
    quad, r = divmod(i, 4)
    pair, half = divmod(quad, 2)
    return pair, 2 * pair + r // 2, 2 * half + r % 2


def t_uses(step):
    out = []
    if step >= 6 and (step - 6) % 4 == 0 and (step - 6) // 4 < QUADS:
        out.append(("r", (step - 6) // 4))
    if 0 <= step - 2 < NH:
        n = step - 2
        out += [("d", n, half) for half in range((n // H) // 4 + 1)]
    if step < NH:
        t, i = divmod(step, H)
        if i == 0 and t > 0:
            out += [("q", t, 6), ("q", t, 7)]
        if t + 1 < NT:
            out += {0: [("x", t + 1)], 8: [("q", t + 1, 0), ("q", t + 1, 1)],
                    9: [("q", t + 1, 2), ("q", t + 1, 3)], 10: [("k", t + 1, 0)],
                    11: [("k", t + 1, 1)], 13: [("q", t + 1, 4), ("q", t + 1, 5)]}.get(i, [])
    return out


T_FIRST = [("x", 0)] + [("q", 0, k) for k in range(4)] + [("k", 0, k) for k in range(2)] + [("q", 0, k) for k in range(4, 8)]
STEPS = NH + 4
T_INDEX = {use: n for n, use in enumerate(T_FIRST + [u for s in range(STEPS) for u in t_uses(s)])}
CHUNKS = (0, 2, 1)
CHUNK_STEP = {1: 0, 3: 2, 10: 1}


def g_index(t, chunk):
    return 3 * t + CHUNKS.index(chunk)


def layer_kernel(nc, x, wq, wk, wv, wo, lq1, lk1, lq2, lk2, gn_w, gn_b, w_up, w_gate, w_down,
                 rope, out):
    x_tiles = x.rearrange("b (t p) d -> b t p d", p=P)
    out_tiles = out.rearrange("b (t p) d -> b t p d", p=P)

    ctx = ExitStack()
    with ctx:
        def sb(name, shape, dt=F32, scope=ctx):
            return scope.enter_context(nc.sbuf_tensor(name, shape, dt))

        sems = []

        def sem(name):
            s = ctx.enter_context(nc.semaphore(name))
            sems.append(s)
            return s

        wbig = sb("wbig", [P, DC * QKV])
        wqkv = wbig[:, :].rearrange("p (c n) -> p c n", c=DC)
        wo_sb = wbig[:, 0:8 * D].rearrange("p (c n) -> p c n", c=8)
        up_t = sb("up_t", [P, DC, E], F8)
        gate_t = sb("gate_t", [P, DC, E], F8)
        down_t = sb("down_t", [P, EB, D], F8)
        attn_t = sb("attn_t", [P, 2, 4, T])
        rope_sb = sb("rope_sb", [P, NT, 4, DH])
        ident = sb("ident", [P, P])
        ident_b = sb("ident_b", [P, P], BF16)
        mask_b = sb("mask_b", [P, P], BF16)
        ones = sb("ones", [P, P])
        blk64 = sb("blk64", [P, P])
        gnw_sb = sb("gnw_sb", [P, 8])
        gnb_sb = sb("gnb_sb", [P, 8])
        neglam = sb("neglam", [P, 1])
        mhalf = sb("mhalf", [P, 8])
        k_silu = sb("k_silu", [P, 1])
        k_hid = sb("k_hid", [P, 1])
        k_out = sb("k_out", [P, 1])
        gstat = sb("gstat", [P, 8, 2, 6])

        S = [ctx.enter_context(nc.psum_tensor(f"S{m}", [P, 2, BANK], F32)) for m in range(2)]
        TB = [ctx.enter_context(nc.psum_tensor(f"TB{m}", [P, BANK], F32)) for m in range(2)]
        PV = ctx.enter_context(nc.psum_tensor("PV", [P, BANK], F32))
        G = ctx.enter_context(nc.psum_tensor("G", [P, BANK], F32))

        def load_qkv(eng, done):
            for c in range(DC):
                rows = slice(c * P, (c + 1) * P)
                for quad in range(4):
                    pair, half = divmod(quad, 2)
                    src = wq[rows, :].rearrange("p (kv j n) -> p kv j n", kv=KV, j=4)
                    eng.dma_start(wqkv[:, c, quad * 256:(quad + 1) * 256].rearrange("p (kv n) -> p kv n", kv=2),
                                  src[:, 2 * pair:2 * pair + 2, 2 * half:2 * half + 2, :]
                                  .rearrange("p kv j n -> p kv (j n)")).then_inc(done, 16)
            eng.dma_start(wqkv[:, :, QC:QC + KC], wk.rearrange("(c p) n -> p c n", p=P)).then_inc(done, 16)
            eng.dma_start(wqkv[:, :, QC + KC:QKV], wv.rearrange("(c p) n -> p c n", p=P)).then_inc(done, 16)
        N_CONST = 13
        N_QKV = 16 * (4 * DC + 2)

        s_wt = [sem(f"s_wt{w}") for w in range(3)]
        s_qkv = sem("s_qkv")
        s_small = sem("s_small")
        s_const = sem("s_const")
        s_abs = sem("s_abs")
        s_tot = sem("s_tot")
        s_totread = sem("s_totread")
        s_tern = sem("s_tern")
        s_ternT = sem("s_ternT")
        s_ternfree = sem("s_ternfree")
        s_lam = sem("s_lam")
        s_lamexp = sem("s_lamexp")
        s_dve0 = sem("s_dve0")
        with ExitStack() as once:
            wt = [sb(f"wt{w}", [P, EB * D], scope=once) for w in range(3)]
            isneg = sb("isneg", [P, 4096], F16, once)
            tern = [sb(f"tern{k}", [P, 4096], F16, once) for k in range(1)]
            ident_h = sb("ident_h", [P, P], F16, once)
            asum = sb("asum", [P, 3], scope=once)
            scale = sb("scale", [P, 3], scope=once)
            thr = sb("thr", [P, 3, 2], scope=once)
            kk = sb("kk", [P, 2], scope=once)
            lamv = sb("lamv", [P, 4, DH], scope=once)
            lamp = sb("lamp", [P, 2, DH], scope=once)
            lams = sb("lams", [P, 2], scope=once)
            lame = sb("lame", [P, 2], scope=once)
            block = once.enter_context(nc.Block())

            @block.sync
            def _(sp):
                for w, src in enumerate((w_up, w_gate)):
                    for half in range(2):
                        sp.dma_start(wt[w][:, half * 4096:(half + 1) * 4096].rearrange("p (e d) -> p e d", d=D),
                                     src.rearrange("(e p) d -> p e d", p=P)[:, half * 8:half * 8 + 8, :])\
                            .then_inc(s_wt[w], 16)
                for half in range(2):
                    sp.dma_start(wt[2][:, half * 4096:(half + 1) * 4096].rearrange("p (c e) -> p c e", e=E),
                                 w_down.rearrange("(c p) e -> p c e", p=P)[:, half * 2:half * 2 + 2, :])\
                        .then_inc(s_wt[2], 16)
                load_qkv(sp, s_qkv)
                sp.wait_ge(s_qkv, N_QKV)

            @block.gpsimd
            def _(pool):
                done = [0]

                def link(ins):
                    done[0] += 1
                    ins.then_inc(s_const, 1)
                    pool.wait_ge(s_const, done[0])

                for m in (ident, ident_b, ident_h, mask_b, blk64):
                    link(nc.gpsimd.memset(m[:, :], 0.0))
                link(nc.gpsimd.memset(ones[:, :], 1.0))
                link(nc.gpsimd.memset(mhalf[:, :], -0.5))
                link(nc.gpsimd.memset(blk64[0:64, 0:64], 1.0 / 64))
                link(nc.gpsimd.memset(blk64[64:128, 64:128], 1.0 / 64))
                for m in (ident, ident_b, ident_h):
                    link(nc.gpsimd.affine_select(out=m[:, :], in_=m[:, :], compare_op=ALU.not_equal, fill=1.0, base=0,
                                                 pattern=[[-1, P]], channel_multiplier=1))
                link(nc.gpsimd.affine_select(out=mask_b[:, :], in_=mask_b[:, :], compare_op=ALU.is_ge, fill=NEG,
                                             base=0, pattern=[[-1, P]], channel_multiplier=1))
                assert done[0] == N_CONST

            @block.scalar
            def _(act):
                for k, v in enumerate((lq1, lk1, lq2, lk2)):
                    act.dma_start(lamv[:, k, :], v.rearrange("(o n) -> o n", o=1).broadcast_to((P, DH)))\
                        .then_inc(s_small, 16)
                act.dma_start(rope_sb[:, :, :, :], rope.rearrange("(t p) f d -> p t f d", p=P)).then_inc(s_small, 16)
                for dst, src in ((gnw_sb, gn_w), (gnb_sb, gn_b)):
                    v = src.rearrange("(pair kv j d o) -> kv d pair j o", pair=2, kv=2, j=4, o=1)
                    for kv in range(2):
                        for pair in range(2):
                            act.dma_start(dst[64 * kv:64 * kv + 64, 4 * pair:4 * pair + 4]
                                          .rearrange("d (j o) -> d j o", o=1), v[kv, :, pair],
                                          allow_slow_non_contiguous=True).then_inc(s_small, 16)
                act.wait_ge(s_lam, 1)
                nc.scalar.activation(lame[:, :], lams[:, :], ACT.Exp).then_inc(s_lamexp, 1)
                for w in range(3):
                    for half in range(2):
                        for b in range(4):
                            n = 8 * w + 4 * half + b
                            act.wait_ge(s_ternT, n + 1)
                            src = TB[n % 2][:, :].bitcast(F16)
                            if w < 2:
                                dst = (up_t, gate_t)[w][:, b, half * 1024:(half + 1) * 1024]
                            else:
                                dst = down_t[:, 4 * b:4 * b + 4, half * 256:(half + 1) * 256]
                                src = src.rearrange("p (e d) -> p e d", e=4)
                            nc.scalar.activation(dst, src, ACT.Copy, saturate=False).then_inc(s_ternfree, 1)

            @block.vector
            def _(dve):
                chain = [0]

                def link(ins):
                    chain[0] += 1
                    ins.then_inc(s_dve0, 1)
                    dve.wait_ge(s_dve0, chain[0])

                dve.wait_ge(s_small, 16 * 13)
                lv = lamv[:, :, :].rearrange("p (a b) d -> p a b d", b=2)
                link(nc.vector.tensor_tensor(lamp[:, :, :], lv[:, :, 0, :], lv[:, :, 1, :], ALU.mult))
                nc.vector.tensor_reduce(lams[:, :], lamp[:, :, :], AX.X, ALU.add).then_inc(s_lam, 1)
                dve.wait_ge(s_lamexp, 1)
                nc.vector.scalar_tensor_tensor(neglam[:, :], lame[:, 1:2], -LAMBDA_INIT, lame[:, 0:1],
                                               ALU.add, ALU.subtract)
                for w in range(3):
                    dve.wait_ge(s_wt[w], 32)
                    nc.vector.tensor_reduce(asum[:, w:w + 1], wt[w][:, :], AX.X, ALU.add,
                                            apply_absolute_value=True).then_inc(s_abs, 1)
                    dve.wait_ge(s_tot, w + 1)
                    link(nc.vector.tensor_scalar(scale[:, w:w + 1], PV[:, w:w + 1], 1.0 / (E * D), TERNARY_EPS,
                                                 ALU.mult, ALU.add))
                    nc.vector.tensor_scalar(thr[:, w, 0:1], scale[:, w:w + 1], 0.5, None, ALU.mult)
                    link(nc.vector.tensor_scalar(thr[:, w, 1:2], scale[:, w:w + 1], -0.5, None, ALU.mult))
                    for half in range(2):
                        n = 2 * w + half
                        src = wt[w][:, half * 4096:(half + 1) * 4096]
                        link(nc.vector.tensor_scalar(isneg[:, :], src, thr[:, w, 1:2], None, ALU.is_lt))
                        if n >= 1:
                            dve.wait_ge(s_ternT, 4 * n)
                        nc.vector.scalar_tensor_tensor(tern[0][:, :], src, thr[:, w, 0:1], isneg[:, :],
                                                       ALU.is_gt, ALU.subtract).then_inc(s_tern, 1)
                        dve.wait_ge(s_tern, n + 1)
                nc.vector.tensor_scalar(k_silu[:, :], scale[:, 0:1], 1.0 / XS, None, ALU.mult)
                link(nc.vector.tensor_scalar(kk[:, 0:1], scale[:, 0:1], XS * HS, None, ALU.mult))
                nc.vector.reciprocal(k_hid[:, :], kk[:, 0:1])
                link(nc.vector.tensor_scalar(kk[:, 1:2], scale[:, 0:1], scale[:, 1:2], HS, ALU.mult, ALU.mult))
                link(nc.vector.tensor_scalar(k_out[:, :], kk[:, 1:2], scale[:, 2:3], None, ALU.mult))

            @block.tensor
            def _(pe):
                pe.wait_ge(s_const, N_CONST)
                for w in range(3):
                    pe.wait_ge(s_abs, w + 1)
                    if w:
                        pe.wait_ge(s_tern, 2 * w)
                    nc.tensor.matmul(PV[:, w:w + 1], ones[:, :], asum[:, w:w + 1], start=True, stop=True)\
                        .then_inc(s_tot, 1)
                    for half in range(2):
                        pe.wait_ge(s_tern, 2 * w + half + 1)
                        for b in range(4):
                            n = 8 * w + 4 * half + b
                            if n >= 2:
                                pe.wait_ge(s_ternfree, n - 1)
                            bank = TB[n % 2][:, :].bitcast(F16)
                            for k in range(8):
                                if w < 2:
                                    at = k * D + b * P
                                else:
                                    at = (k % 2) * E + (4 * b + k // 2) * P
                                last = nc.tensor.transpose(bank[:, k * P:(k + 1) * P], tern[0][:, at:at + P],
                                                           ident_h[:, :])
                            last.then_inc(s_ternT, 1)

        s_xin = [sem(f"s_xin{k}") for k in range(2)]
        s_wo = sem("s_wo")
        s_tfull = sem("s_tfull")
        s_tfree = sem("s_tfree")
        s_gfull = sem("s_gfull")
        s_gfree = sem("s_gfree")
        s_hl = sem("s_hl")
        s_score = sem("s_score")
        s_negmax = sem("s_negmax")
        s_exp = sem("s_exp")
        s_comb = sem("s_comb")
        s_diag = sem("s_diag")
        s_pv = sem("s_pv")
        s_pvfree = sem("s_pvfree")
        s_dve = sem("s_dve")
        s_xr = [sem(f"s_xr{k}") for k in range(4)]
        s_gst = sem("s_gst")
        s_mv = sem("s_mv")
        s_gm = sem("s_gm")
        s_gv = sem("s_gv")
        s_gvm = sem("s_gvm")
        s_gr = sem("s_gr")
        s_grs = sem("s_grs")
        s_aff = sem("s_aff")
        s_nv = sem("s_nv")
        s_na = sem("s_na")
        s_y = sem("s_y")
        s_yfree = sem("s_yfree")
        s_var = sem("s_var")
        s_eps = sem("s_eps")
        s_rstd = sem("s_rstd")
        s_x1 = sem("s_x1")
        s_x1T = sem("s_x1T")
        s_xhi = sem("s_xhi")
        s_xlo = sem("s_xlo")
        s_ug = sem("s_ug")
        s_sl = sem("s_sl")
        s_h = sem("s_h")
        s_hhi = sem("s_hhi")
        s_hlo = sem("s_hlo")
        s_ready = sem("s_ready")
        s_od = [sem(f"s_od{k}") for k in range(2)]
        s_qkv2 = sem("s_qkv2")
        s_dve2 = sem("s_dve2")
        round_sems = sems[sems.index(s_xin[0]):]

        with nc.Fori(0, B) as b:
            with ExitStack() as att:
                xt = sb("xt", [P, 2, D], scope=att)
                x_t = sb("x_t", [P, DC, P], scope=att)
                t1 = sb("t1", [P, BANK], scope=att)
                t2 = sb("t2", [P, BANK], scope=att)
                hl = sb("hl", [P, 24, 4, DH], scope=att)
                qstk = sb("qstk", [P, 32, P], F32R, att)
                kstk = sb("kstk", [P, 8, T], F32R, att)
                v_sb = sb("v_sb", [P, NT, KC], scope=att)
                e1 = [sb(f"e1_{k}", [P, T], scope=att) for k in range(3)]
                e2 = [sb(f"e2_{k}", [P, T], scope=att) for k in range(2)]
                nmax = sb("nmax", [P, 4], scope=att)
                lsum = sb("lsum", [P, 2, 2], scope=att)
                linv = sb("linv", [P, 8, 2], scope=att)
                coef = sb("coef", [P, 2], scope=att)
                diag = sb("diag", [P, 4, P], scope=att)
                dt_sb = sb("dt_sb", [P, NT, 4, P], scope=att)
                r_sb = sb("r_sb", [P, 2, P], scope=att)
                block = att.enter_context(nc.Block())

                def halves(t):
                    w = (t + 1) * P
                    return (1, w) if w <= BANK else (2, w // 2)

                @block.sync
                def _(sp):
                    for t in range(NT):
                        if t >= 2:
                            sp.wait_ge(s_tfull, T_INDEX["x", t - 2] + 1)
                        sp.dma_start(xt[:, t % 2, :], x_tiles[bass.ds(b, 1), t].rearrange("o p d -> p (o d)"))\
                            .then_inc(s_xin[t % 2], 16)
                    sp.wait_ge(s_gfree, 3 * NT)
                    wo_v = wo.rearrange("(pair kv j d) n -> kv d pair j n", pair=2, kv=2, j=4)
                    for kv in range(2):
                        for pair in range(2):
                            sp.dma_start(wo_sb[64 * kv:64 * kv + 64, 4 * pair:4 * pair + 4, :], wo_v[kv, :, pair])\
                                .then_inc(s_wo, 16)
                    sp.wait_ge(s_wo, 64)

                @block.tensor
                def _(pe):
                    def t_bank(use):
                        n = T_INDEX[use]
                        if n >= 2:
                            pe.wait_ge(s_tfree, n - 1)
                        return TB[n % 2]

                    def fill(use):
                        kind = use[0]
                        if kind == "x":
                            t = use[1]
                            pe.wait_ge(s_xin[t % 2], 16 * (t // 2 + 1))
                            bank = t_bank(use)
                            for c in range(DC):
                                last = nc.tensor.transpose(bank[:, c * P:(c + 1) * P],
                                                           xt[:, t % 2, c * P:(c + 1) * P], ident[:, :])
                        elif kind in "qk":
                            _, t, k = use
                            chunk = 2 if kind == "k" else k // 4
                            pe.wait_ge(s_hl, g_index(t, chunk) + 1)
                            bank = t_bank(use)
                            for m in range(4):
                                row = 16 + 4 * k + m if kind == "k" else 4 * (k % 4) + m
                                last = nc.tensor.transpose(bank[:, m * P:(m + 1) * P],
                                                           hl[:, row, :, :].rearrange("p a d -> p (a d)"), ident[:, :])
                        elif kind == "d":
                            _, n, half = use
                            pe.wait_ge(s_comb, n + 1)
                            bank = t_bank(use)
                            for k in range(min(4, n // H + 1 - 4 * half)):
                                at = (4 * half + k) * P
                                last = nc.tensor.transpose(bank[:, k * P:(k + 1) * P], e1[n % 3][:, at:at + P],
                                                           ident[:, :])
                        else:
                            pe.wait_ge(s_diag, use[1] + 1)
                            bank = t_bank(use)
                            for kv in range(2):
                                last = nc.tensor.matmul(bank[64 * kv:64 * kv + 64, 0:256], ones[:, 0:64],
                                                        diag[:, 2 * kv:2 * kv + 2, :].rearrange("p a q -> p (a q)"),
                                                        start=True, stop=True)
                        last.then_inc(s_tfull, 1)

                    def project(t, chunk):
                        g = g_index(t, chunk)
                        pe.wait_ge(s_tfree, T_INDEX["x", t] + 1)
                        if g:
                            pe.wait_ge(s_gfree, g)
                        for c in range(DC):
                            last = nc.tensor.matmul(G[:, :], x_t[:, c, :], wqkv[:, c, chunk * BANK:(chunk + 1) * BANK],
                                                    start=c == 0, stop=c == DC - 1)
                        last.then_inc(s_gfull, 1)

                    def scores(n):
                        t, i = divmod(n, H)
                        _, kv, _ = head_of(i)
                        parts, w = halves(t)
                        pe.wait_ge(s_tfree, T_INDEX["q", t, i // 2] + 1)
                        pe.wait_ge(s_tfree, T_INDEX["k", t, kv // 2] + 1)
                        for m in range(2):
                            if n:
                                pe.wait_ge(s_exp, 2 * n + m - 1)
                            for h in range(parts):
                                nc.tensor.matmul(S[m][:, h, 0:w], qstk[:, 2 * i + m, :],
                                                 kstk[:, 2 * kv + m, h * w:(h + 1) * w],
                                                 start=True, stop=h < parts - 1)
                            nc.tensor.matmul(S[m][:, parts - 1, w - P:w], ident_b[:, :], mask_b[:, :],
                                             start=False, stop=True).then_inc(s_score, 1)

                    def values(quad):
                        t = quad // 4
                        pair = (quad % 4) // 2
                        pe.wait_ge(s_gfree, g_index(t, 2) + 1)
                        pe.wait_ge(s_tfree, T_INDEX["d", 4 * quad + 3, t // 4] + 1)
                        if quad:
                            pe.wait_ge(s_pvfree, quad)
                        for kb in range(t + 1):
                            for kv in range(2):
                                at = (2 * pair + kv) * 2 * DH
                                last = nc.tensor.matmul(
                                    PV[64 * kv:64 * kv + 64, 0:256], v_sb[:, kb, at:at + 2 * DH],
                                    dt_sb[:, kb, 2 * kv:2 * kv + 2, :].rearrange("p a q -> p (a q)"),
                                    start=kb == 0, stop=kb == t)
                        last.then_inc(s_pv, 1)

                    fill(("x", 0))
                    for chunk in CHUNKS[:2]:
                        project(0, chunk)
                    for use in T_FIRST[1:7]:
                        fill(use)
                    project(0, CHUNKS[2])
                    for use in T_FIRST[7:]:
                        fill(use)
                    for step in range(STEPS):
                        if step < NH:
                            scores(step)
                        if step >= 6 and (step - 6) % 4 == 0 and (step - 6) // 4 < QUADS:
                            values((step - 6) // 4)
                        for use in t_uses(step):
                            fill(use)
                        t, i = divmod(step, H)
                        if t + 1 < NT and i in CHUNK_STEP:
                            project(t + 1, CHUNK_STEP[i])

                @block.scalar
                def _(act):
                    def copy_out(use):
                        n = T_INDEX[use]
                        kind = use[0]
                        src = TB[n % 2]
                        act.wait_ge(s_tfull, n + 1)
                        if kind == "x":
                            t = use[1]
                            if t:
                                act.wait_ge(s_gfull, 3 * t)
                            dst = x_t[:, :, :]
                            src = src[:, :].rearrange("p (c q) -> p c q", c=DC)
                        elif kind == "q":
                            k = use[2]
                            dst = qstk[:, 4 * k:4 * k + 4, :]
                            src = src[:, :].rearrange("p (m q) -> p m q", m=4)
                        elif kind == "k":
                            _, t, k = use
                            dst = kstk[:, 4 * k:4 * k + 4, t * P:(t + 1) * P]
                            src = src[:, :].rearrange("p (m q) -> p m q", m=4)
                        elif kind == "d":
                            _, n, half = use
                            blocks = min(4, n // H + 1 - 4 * half)
                            if n // 4:
                                act.wait_ge(s_pv, n // 4)
                            dst = dt_sb[:, 4 * half:4 * half + blocks, n % 4, :]
                            src = src[:, 0:blocks * P].rearrange("p (k q) -> p k q", q=P)
                        else:
                            if use[1]:
                                act.wait_ge(s_pvfree, use[1])
                            dst = r_sb[:, :, :]
                            src = src[:, 0:256].rearrange("p (a q) -> p a q", a=2)
                        nc.scalar.activation(dst, src, ACT.Copy).then_inc(s_tfree, 1)

                    for use in T_FIRST:
                        copy_out(use)
                    for step in range(STEPS):
                        if step < NH:
                            n = step
                            parts, w = halves(n // H)
                            for m in range(2):
                                act.wait_ge(s_negmax, 2 * n + m + 1)
                                if m == 0 and n >= 3:
                                    act.wait_ge(s_tfull, T_INDEX["d", n - 3, (n - 3) // H // 4] + 1)
                                if n >= 2:
                                    act.wait_ge(s_comb, n - 1)
                                e = (e1[n % 3], e2[n % 2])[m]
                                nc.scalar.activation(e[:, 0:parts * w].rearrange("p (h w) -> p h w", h=parts),
                                                     S[m][:, 0:parts, 0:w], ACT.Exp,
                                                     bias=nmax[:, (2 * n + m) % 4:(2 * n + m) % 4 + 1], scale=1.0,
                                                     accum_out=lsum[:, n % 2, m:m + 1]).then_inc(s_exp, 1)
                        for use in t_uses(step):
                            copy_out(use)

                @block.vector
                def _(dve):
                    chain = [0]

                    def link(ins):
                        chain[0] += 1
                        ins.then_inc(s_dve, 1)
                        dve.wait_ge(s_dve, chain[0])

                    def rotate(t, chunk):
                        g = g_index(t, chunk)
                        maps = 8 if chunk == 2 else 16
                        at = 16 if chunk == 2 else 0
                        cols = maps * DH
                        f = 2 if chunk == 2 else 0
                        cos = rope_sb[:, t, f:f + 1, :].broadcast_to((P, maps, DH))
                        sin = rope_sb[:, t, f + 1:f + 2, :].rearrange("p o (i s) -> p o i s", s=2)\
                            .broadcast_to((P, maps, DH // 2, 2))
                        a, c = t1[:, 0:cols], t2[:, 0:cols]
                        if g:
                            dve.wait_ge(s_hl, g)
                        dve.wait_ge(s_gfull, g + 1)
                        if chunk == 2:
                            nc.vector.tensor_copy(v_sb[:, t, :], G[:, KC:2 * KC])
                        nc.vector.tensor_tensor(a.rearrange("p (m d) -> p m d", d=DH),
                                                G[:, 0:cols].rearrange("p (m d) -> p m d", d=DH), cos, ALU.mult)
                        nc.vector.tensor_tensor(c.rearrange("p (m i s) -> p m i s", i=DH // 2, s=2),
                                                G[:, 0:cols].rearrange("p (m i s) -> p m i s", i=DH // 2, s=2)
                                                [:, :, :, ::-1], sin, ALU.mult).then_inc(s_gfree, 1)
                        dve.wait_ge(s_gfree, g + 1)
                        link(nc.vector.tensor_tensor(a, a, c, ALU.add))
                        before = {0: ("q", t - 1, 7), 1: ("q", t, 3), 2: ("k", t - 1, 1)}[chunk]
                        if before in T_INDEX:
                            dve.wait_ge(s_tfull, T_INDEX[before] + 1)
                        rows = hl[:, at:at + maps, :, :]
                        hi, lo = ((rows[:, :, 0:4:2, :], rows[:, :, 1:4:2, :]) if chunk == 2 else
                                  (rows[:, :, 0:2, :], rows[:, :, 2:4, :]))
                        twice = a.rearrange("p (m o d) -> p m o d", o=1, d=DH).broadcast_to((P, maps, 2, DH))
                        link(nc.vector.tensor_scalar(hi.bitcast(I32), twice.bitcast(I32), HI_BITS, None,
                                                     ALU.bitwise_and))
                        nc.vector.tensor_tensor(lo, twice, hi, ALU.subtract).then_inc(s_hl, 1)

                    def neg_max(n, m):
                        parts, w = halves(n // H)
                        u = 2 * n + m
                        dve.wait_ge(s_score, u + 1)
                        nc.vector.tensor_reduce(nmax[:, u % 4:u % 4 + 1], S[m][:, 0:parts, 0:w], AX.XY, ALU.max,
                                                negate=True).then_inc(s_negmax, 1)

                    for chunk in CHUNKS:
                        rotate(0, chunk)
                    for step in range(STEPS):
                        n = step - 1
                        if 0 <= n < NH:
                            dve.wait_ge(s_exp, 2 * n + 2)
                            nc.vector.reciprocal(linv[:, n % 8, :], lsum[:, n % 2, :]).then_inc(s_dve, 1)
                            chain[0] += 1
                            recip = chain[0]
                        if step < NH:
                            neg_max(step, 0)
                        if 0 <= n < NH:
                            dve.wait_ge(s_dve, recip)
                            nc.vector.tensor_scalar(coef[:, n % 2:n % 2 + 1], lsum[:, n % 2, 0:1], linv[:, n % 8, 1:2],
                                                    neglam[:, :], ALU.mult, ALU.mult).then_inc(s_dve, 1)
                            chain[0] += 1
                            coefed = chain[0]
                        if step < NH:
                            neg_max(step, 1)
                        if 0 <= n < NH:
                            w = (n // H + 1) * P
                            dve.wait_ge(s_dve, coefed)
                            nc.vector.scalar_tensor_tensor(e1[n % 3][:, 0:w], e2[n % 2][:, 0:w],
                                                           coef[:, n % 2:n % 2 + 1], e1[n % 3][:, 0:w],
                                                           ALU.mult, ALU.add).then_inc(s_comb, 1)
                            if n % 4 == 3:
                                quad = n // 4
                                if quad:
                                    dve.wait_ge(s_tfull, T_INDEX["r", quad - 1] + 1)
                                nc.vector.tensor_tensor(
                                    diag[:, :, :], ident[:, :].rearrange("p (o q) -> p o q", o=1).broadcast_to((P, 4, P)),
                                    linv[:, (n - 3) % 8:(n - 3) % 8 + 4, 0:1].broadcast_to((P, 4, P)),
                                    ALU.mult).then_inc(s_diag, 1)
                        if step >= 7 and (step - 7) % 4 == 0:
                            quad = (step - 7) // 4
                            t, (pair, half) = quad // 4, divmod(quad % 4, 2)
                            dve.wait_ge(s_tfree, T_INDEX["r", quad] + 1)
                            dve.wait_ge(s_pv, quad + 1)
                            nc.vector.tensor_tensor(attn_t[:, pair, 2 * half:2 * half + 2, t * P:(t + 1) * P],
                                                    PV[:, 0:256].rearrange("p (a q) -> p a q", a=2), r_sb[:, :, :],
                                                    ALU.mult).then_inc(s_pvfree, 1)
                        t, i = divmod(step, H)
                        if t + 1 < NT and i - 1 in CHUNK_STEP:
                            rotate(t + 1, CHUNK_STEP[i - 1])
                        if t == 4 and 6 <= i < 14:
                            if i == 6:
                                dve.wait_ge(s_pvfree, 16)
                            j = i - 6
                            nc.vector.bn_stats(gstat[:, j, 0, :], attn_t[:, j // 4, j % 4, 0:T // 2])

            with ExitStack() as mix:
                x1 = sb("x1", [P, NT, D], scope=mix)
                x1_hi = sb("x1_hi", [P, DC, T], F16, mix)
                x1_lo = sb("x1_lo", [P, DC, T], F16, mix)
                hid_hi = sb("hid_hi", [P, EB, BANK], F16, mix)
                hid_lo = sb("hid_lo", [P, EB, BANK], F16, mix)
                sl = sb("sl", [P, 2, BANK], scope=mix)
                hh = sb("hh", [P, 2, BANK], scope=mix)
                z = sb("z", [P, 2, D], scope=mix)
                mv = sb("mv", [P, 8, 2], scope=mix)
                gm = sb("gm", [P, 8], scope=mix)
                dm = sb("dm", [P, 8], scope=mix)
                rv = sb("rv", [P, 8], scope=mix)
                gv = sb("gv", [P, 8], scope=mix)
                rs = sb("rs", [P, 8], scope=mix)
                fac = sb("fac", [P, 8], scope=mix)
                off = sb("off", [P, 8], scope=mix)
                lst = sb("lst", [P, 2, 6], scope=mix)
                lmv = sb("lmv", [P, 2, 2], scope=mix)
                lrs = sb("lrs", [P, 2], scope=mix)
                block = mix.enter_context(nc.Block())
                Y = [PV, G]
                NF = 2 * EB
                NY = 2 * NT

                @block.sync
                def _(sp):
                    for k in range(4):
                        sp.dma_start(x1[:, 2 * k:2 * k + 2, :],
                                     x_tiles[bass.ds(b, 1), 2 * k:2 * k + 2].rearrange("o t p d -> p (o t) d"))\
                            .then_inc(s_xr[k], 16)
                    sp.wait_ge(s_y, NT)
                    load_qkv(sp, s_qkv2)
                    for k in range(NT):
                        sp.wait_ge(s_ready, k + 1)
                        sp.dma_start(out_tiles[bass.ds(b, 1), k].rearrange("o p d -> p (o d)"), z[:, k % 2, :])\
                            .then_inc(s_od[k % 2], 16)
                    for k in range(2):
                        sp.wait_ge(s_od[k], 16 * (NT // 2))
                    sp.wait_ge(s_qkv2, N_QKV)

                @block.gpsimd
                def _(pool):
                    pool.wait_ge(s_gr, 1)
                    nc.gpsimd.tensor_scalar(gv[:, :], gv[:, :], LN_EPS, None, ALU.add).then_inc(s_eps, 1)
                    pool.wait_ge(s_eps, 1)
                    nc.gpsimd.tensor_tensor(rs[:, :], gv[:, :], mhalf[:, :], ALU.pow).then_inc(s_grs, 1)
                    for k in range(NY):
                        pool.wait_ge(s_var, k + 1)
                        veps = lmv[:, k % 2, 1:2]
                        nc.gpsimd.tensor_scalar(veps, veps, LN_EPS, None, ALU.add).then_inc(s_eps, 1)
                        pool.wait_ge(s_eps, k + 2)
                        nc.gpsimd.tensor_tensor(lrs[:, k % 2:k % 2 + 1], veps, mhalf[:, 0:1], ALU.pow)\
                            .then_inc(s_rstd, 1)

                @block.tensor
                def _(pe):
                    def x1_transposed(k):
                        pe.wait_ge(s_x1, k + 1)
                        if k >= 2:
                            pe.wait_ge(s_xlo, k - 1)
                        for c in range(DC):
                            last = nc.tensor.transpose(TB[k % 2][:, c * P:(c + 1) * P], x1[:, k, c * P:(c + 1) * P],
                                                       ident[:, :])
                        last.then_inc(s_x1T, 1)

                    def up_gate(f):
                        ch, eb = divmod(f, EB)
                        if f == 0:
                            pe.wait_ge(s_xlo, 4)
                        if f == EB:
                            pe.wait_ge(s_xlo, 8)
                        if f >= 2:
                            pe.wait_ge(s_h, f - 1)
                        for k, w in enumerate((up_t, gate_t)):
                            for c in range(DC):
                                for part in (x1_hi, x1_lo):
                                    last = nc.tensor.matmul(S[f % 2][:, k, :], w[:, c, eb * P:(eb + 1) * P],
                                                            part[:, c, ch * BANK:(ch + 1) * BANK],
                                                            start=c == 0 and part is x1_hi,
                                                            stop=c == DC - 1 and part is x1_lo)
                        last.then_inc(s_ug, 1)

                    pe.wait_ge(s_mv, 1)
                    nc.tensor.matmul(TB[0][:, 0:8], blk64[:, :], mv[:, :, 0], start=True, stop=True).then_inc(s_gm, 1)
                    pe.wait_ge(s_gv, 1)
                    nc.tensor.matmul(TB[1][:, 0:8], blk64[:, :], rv[:, :], start=True, stop=True).then_inc(s_gvm, 1)
                    for k in range(NT):
                        half = k // 4
                        pe.wait_ge(s_nv, 4 * half + 4)
                        pe.wait_ge(s_na, 4 * half + 4)
                        if k >= 2:
                            pe.wait_ge(s_yfree, k - 1)
                        for c in range(8):
                            last = nc.tensor.matmul(Y[k % 2][:, :], attn_t[:, c // 4, c % 4, k * P:(k + 1) * P],
                                                    wo_sb[:, c, :], start=c == 0, stop=c == 7)
                        last.then_inc(s_y, 1)
                        if k >= 2:
                            x1_transposed(k - 2)
                    up_gate(0)
                    x1_transposed(NT - 2)
                    x1_transposed(NT - 1)
                    for ch in range(2):
                        for eb in range(EB):
                            if ch or eb:
                                up_gate(ch * EB + eb)
                        for j in range(4):
                            y = NT + 4 * ch + j
                            pe.wait_ge(s_yfree, y - 1)
                            for eb in range(EB):
                                if j == 0:
                                    pe.wait_ge(s_hlo, ch * EB + eb + 1)
                                for part in (hid_hi, hid_lo):
                                    last = nc.tensor.matmul(Y[y % 2][:, :], part[:, eb, j * P:(j + 1) * P],
                                                            down_t[:, eb, :], start=eb == 0 and part is hid_hi,
                                                            stop=eb == EB - 1 and part is hid_lo)
                            last.then_inc(s_y, 1)

                @block.scalar
                def _(act):
                    def x1_high(k):
                        act.wait_ge(s_x1T, k + 1)
                        nc.scalar.activation(x1_hi[:, :, k * P:(k + 1) * P],
                                             TB[k % 2][:, :].rearrange("p (c q) -> p c q", c=DC),
                                             ACT.Copy, scale=XS).then_inc(s_xhi, 1)

                    def hidden_high(f):
                        act.wait_ge(s_h, f + 1)
                        if f >= EB and f % EB == 0:
                            act.wait_ge(s_y, NT + 4 * (f // EB))
                        nc.scalar.activation(hid_hi[:, f % EB, :], hh[:, f % 2, :], ACT.Copy).then_inc(s_hhi, 1)

                    act.wait_ge(s_aff, 1)
                    for half in range(2):
                        for j in range(4, 8):
                            v = attn_t[:, j // 4, j % 4, half * BANK:(half + 1) * BANK]
                            nc.scalar.activation(v, v, ACT.Identity, bias=off[:, j:j + 1], scale=fac[:, j:j + 1])\
                                .then_inc(s_na, 1)
                    for k in range(NT - 2):
                        x1_high(k)
                    for f in range(NF):
                        act.wait_ge(s_ug, f + 1)
                        if f >= 2:
                            act.wait_ge(s_h, f - 1)
                        nc.scalar.activation(sl[:, f % 2, :], S[f % 2][:, 0, :], ACT.Silu, scale=k_silu[:, :])\
                            .then_inc(s_sl, 1)
                        if f == 0:
                            x1_high(NT - 2)
                            x1_high(NT - 1)
                        if f % EB:
                            hidden_high(f - 1)
                        if f % EB == EB - 1:
                            hidden_high(f)

                @block.vector
                def _(dve):
                    chain = [0]

                    def link(ins):
                        chain[0] += 1
                        ins.then_inc(s_dve2, 1)
                        dve.wait_ge(s_dve2, chain[0])

                    def variance(k, v):
                        link(nc.vector.bn_stats(lst[:, k % 2, :], v))
                        nc.vector.bn_aggr(lmv[:, k % 2, :], lst[:, k % 2, :]).then_inc(s_var, 1)

                    def normalised(k, v):
                        dve.wait_ge(s_rstd, k + 1)
                        return nc.vector.tensor_scalar(v, v, lmv[:, k % 2, 0:1], lrs[:, k % 2:k % 2 + 1],
                                                       ALU.subtract, ALU.mult)

                    def x1_low(k):
                        dve.wait_ge(s_xhi, k + 1)
                        nc.vector.scalar_tensor_tensor(x1_lo[:, :, k * P:(k + 1) * P],
                                                       TB[k % 2][:, :].rearrange("p (c q) -> p c q", c=DC), XS,
                                                       x1_hi[:, :, k * P:(k + 1) * P], ALU.mult, ALU.subtract)\
                            .then_inc(s_xlo, 1)

                    def hidden_low(f):
                        dve.wait_ge(s_hhi, f + 1)
                        nc.vector.tensor_tensor(hid_lo[:, f % EB, :], hh[:, f % 2, :], hid_hi[:, f % EB, :],
                                                ALU.subtract).then_inc(s_hlo, 1)

                    for j in range(8):
                        last = nc.vector.bn_stats(gstat[:, j, 1, :], attn_t[:, j // 4, j % 4, T // 2:T])
                    last.then_inc(s_gst, 1)
                    dve.wait_ge(s_gst, 1)
                    for j in range(8):
                        last = nc.vector.bn_aggr(mv[:, j, :], gstat[:, j, :, :].rearrange("p h s -> p (h s)"))
                    last.then_inc(s_mv, 1)
                    dve.wait_ge(s_gm, 1)
                    nc.vector.tensor_copy(gm[:, :], TB[0][:, 0:8])
                    dve.wait_ge(s_mv, 1)
                    link(nc.vector.tensor_tensor(dm[:, :], mv[:, :, 0], TB[0][:, 0:8], ALU.subtract))
                    link(nc.vector.tensor_tensor(dm[:, :], dm[:, :], dm[:, :], ALU.mult))
                    nc.vector.tensor_tensor(rv[:, :], dm[:, :], mv[:, :, 1], ALU.add).then_inc(s_gv, 1)
                    dve.wait_ge(s_gvm, 1)
                    nc.vector.tensor_copy(gv[:, :], TB[1][:, 0:8]).then_inc(s_gr, 1)
                    dve.wait_ge(s_grs, 1)
                    link(nc.vector.tensor_tensor(fac[:, :], gnw_sb[:, :], rs[:, :], ALU.mult))
                    link(nc.vector.tensor_scalar(fac[:, :], fac[:, :], 1.0 - LAMBDA_INIT, None, ALU.mult))
                    link(nc.vector.tensor_tensor(dm[:, :], gm[:, :], fac[:, :], ALU.mult))
                    nc.vector.scalar_tensor_tensor(off[:, :], gnb_sb[:, :], 1.0 - LAMBDA_INIT, dm[:, :],
                                                   ALU.mult, ALU.subtract).then_inc(s_aff, 1)
                    dve.wait_ge(s_aff, 1)
                    for half in range(2):
                        for j in range(4):
                            v = attn_t[:, j // 4, j % 4, half * BANK:(half + 1) * BANK]
                            nc.vector.tensor_scalar(v, v, fac[:, j:j + 1], off[:, j:j + 1], ALU.mult, ALU.add)\
                                .then_inc(s_nv, 1)

                    for k in range(NT + 1):
                        if k < NT:
                            dve.wait_ge(s_xr[k // 2], 16)
                            dve.wait_ge(s_y, k + 1)
                            nc.vector.tensor_tensor(x1[:, k, :], Y[k % 2][:, :], x1[:, k, :], ALU.add)\
                                .then_inc(s_yfree, 1)
                            dve.wait_ge(s_yfree, k + 1)
                            variance(k, x1[:, k, :])
                        if k >= 1:
                            normalised(k - 1, x1[:, k - 1, :]).then_inc(s_x1, 1)
                        if k >= 3:
                            x1_low(k - 3)

                    for ch in range(2):
                        for eb in range(EB):
                            f = ch * EB + eb
                            dve.wait_ge(s_sl, f + 1)
                            if f >= 2:
                                dve.wait_ge(s_hhi, f - 1)
                                dve.wait_ge(s_hlo, f - 1)
                            nc.vector.scalar_tensor_tensor(hh[:, f % 2, :], sl[:, f % 2, :], k_hid[:, :],
                                                           S[f % 2][:, 1, :], ALU.mult, ALU.mult).then_inc(s_h, 1)
                            if f == 0:
                                x1_low(NT - 2)
                                x1_low(NT - 1)
                            if eb:
                                hidden_low(f - 1)
                        hidden_low(ch * EB + EB - 1)
                        for j in range(4):
                            k = 4 * ch + j
                            y = NT + k
                            v = z[:, k % 2, :]
                            dve.wait_ge(s_y, y + 1)
                            if k >= 2:
                                dve.wait_ge(s_od[k % 2], 16 * (k // 2))
                            nc.vector.scalar_tensor_tensor(v, Y[y % 2][:, :], k_out[:, :], x1[:, k, :],
                                                           ALU.mult, ALU.add).then_inc(s_yfree, 1)
                            dve.wait_ge(s_yfree, y + 1)
                            variance(y, v)
                            normalised(y, v).then_inc(s_ready, 1)

            nc.all_engine_barrier()
            for s in round_sems:
                nc.sync.sem_clear(s)
            nc.all_engine_barrier()


_INS = ["x", "Wq", "Wk", "Wv", "Wo", "lambda_q1", "lambda_k1", "lambda_q2", "lambda_k2", "gn_w", "gn_b"]


def rope_table():
    inv = (1.0 / np.float32(10000.0) ** (np.arange(0, DH, 2, dtype=np.float32) / np.float32(DH))).astype(np.float32)
    freqs = np.arange(T, dtype=np.float32)[:, None] * inv[None, :]
    cos = np.repeat(np.cos(freqs), 2, axis=1)
    sin = np.repeat(np.sin(freqs), 2, axis=1) * np.tile(np.array([-1.0, 1.0], np.float32), DH // 2)
    s = np.float32(1.0 / math.sqrt(DH))
    return np.ascontiguousarray(np.stack([cos * s, sin * s, cos, sin], axis=1).astype(np.float32))


def kernel(**inputs):
    import concourse.bacc as bacc
    from concourse.bass_utils import run_bass_kernel_spmd

    nc = bacc.Bacc("TRN2", target_bir_lowering=False, num_devices=1)
    named = [("L0_attn_" + n) for n in _INS] + ["L0_ffn_W_up", "L0_ffn_W_gate", "L0_ffn_W_down"]
    arrays = {f"in_{n}": np.ascontiguousarray(inputs[n]) for n in named}
    arrays["in_rope"] = rope_table()
    args = [nc.dram_tensor(n, a.shape, mybir.dt.from_np(a.dtype), kind="ExternalInput").ap() for n, a in arrays.items()]
    args.append(nc.dram_tensor("out", (B, T, D), F32, kind="ExternalOutput").ap())
    layer_kernel(nc, *args)
    r = run_bass_kernel_spmd(nc, [arrays], core_ids=[0])
    return r.results[0]["out"]
```

```python
import math
from contextlib import ExitStack

import numpy as np
import concourse.bass as bass
from concourse import mybir

F32, F32R, F16, BF16 = mybir.dt.float32, mybir.dt.float32r, mybir.dt.float16, mybir.dt.bfloat16
F8, I32 = mybir.dt.float8e4, mybir.dt.int32
ACT = mybir.ActivationFunctionType
ALU = mybir.AluOpType
AX = mybir.AxisListType

B, T, D = 4, 1024, 512
H, KV, DH = 16, 4, 32
E = 2048
P = 128
NT = T // P
DC = D // P
EB = E // P
QC = H * 2 * DH
KC = KV * 2 * DH
QKV = QC + 2 * KC
BANK = 512
NH = NT * H
DUOS = NH // 2
LAMBDA_INIT = 0.8 - 0.6 * math.exp(-0.3 * 0)
LN_EPS = 1e-5
TERNARY_EPS = 1e-8
NEG = -3.0e38
HI_BITS = -4096
XS = 1024.0
HS = 8.0


def head_of(i):
    duo, r = divmod(i, 2)
    pair, j = divmod(duo, 4)
    return pair, 2 * pair + r, j


PROJECT_STEP = {1 + c: (0, c) for c in range(4)} | {6 + c: (2, c) for c in range(4)} | \
    {11 + c: (1, c) for c in range(4)}
ROTATE_STEP = {5: (0, 0), 6: (0, 1), 7: (0, 2), 10: (2, 0), 11: (2, 1), 12: (2, 2), 15: (1, 0)}
ROTATE_LATE = {0: (1, 1), 1: (1, 2)}
PARTS_STEP = {0: ("x", 0), 8: ("q", 0), 9: ("q", 1), 10: ("q", 2), 11: ("q", 3), 13: ("k", 0), 14: ("k", 1)}
PARTS_LATE = {2: ("q", 4), 3: ("q", 5), 4: ("q", 6), 5: ("q", 7)}


def t_uses(step, m):
    out = []
    n = step - 2
    if 0 <= n < NH and 4 * m < n // H + 1:
        out.append(("d", n, m))
    if step < NH and m == 1:
        t, i = divmod(step, H)
        if t > 0 and i in PARTS_LATE:
            out.append((PARTS_LATE[i][0], t, PARTS_LATE[i][1]))
        if t + 1 < NT and i in PARTS_STEP:
            out.append((PARTS_STEP[i][0], t + 1, PARTS_STEP[i][1]))
    return out


T_FIRST = [("x", 0, 0)] + [("q", 0, k) for k in range(4)] + [("k", 0, k) for k in range(2)] + \
    [("q", 0, k) for k in range(4, 8)]
STEPS = NH + 6
T_INDEX = {use: n for n, use in enumerate(T_FIRST + [u for s in range(STEPS) for m in range(2) for u in t_uses(s, m)])}
CHUNKS = (0, 2, 1)


def g_index(t, chunk):
    return 3 * t + CHUNKS.index(chunk)


def layer_kernel(nc, x, wq, wk, wv, wo, lq1, lk1, lq2, lk2, gn_w, gn_b, w_up, w_gate, w_down,
                 rope, out):
    x_tiles = x.rearrange("b (t p) d -> b t p d", p=P)
    out_tiles = out.rearrange("b (t p) d -> b t p d", p=P)

    ctx = ExitStack()
    with ctx:
        def sb(name, shape, dt=F32, scope=ctx):
            return scope.enter_context(nc.sbuf_tensor(name, shape, dt))

        sems = []

        def sem(name):
            s = ctx.enter_context(nc.semaphore(name))
            sems.append(s)
            return s

        wbig = sb("wbig", [P, DC * QKV])
        wqkv = wbig[:, :].rearrange("p (c n) -> p c n", c=DC)
        wo_sb = wbig[:, 0:8 * D].rearrange("p (c n) -> p c n", c=8)
        up_t = sb("up_t", [P, DC, E], F8)
        gate_t = sb("gate_t", [P, DC, E], F8)
        down_t = sb("down_t", [P, EB, D], F8)
        attn_t = sb("attn_t", [P, 2, 4, T])
        rope_sb = sb("rope_sb", [P, NT, 4, DH])
        ident = sb("ident", [P, P])
        ident_b = sb("ident_b", [P, P], BF16)
        mask_b = sb("mask_b", [P, P], BF16)
        ones = sb("ones", [P, P])
        blk64 = sb("blk64", [P, P])
        gnw_sb = sb("gnw_sb", [P, 8])
        gnb_sb = sb("gnb_sb", [P, 8])
        neglam = sb("neglam", [P, 1])
        mhalf = sb("mhalf", [P, 8])
        k_silu = sb("k_silu", [P, 1])
        k_hid = sb("k_hid", [P, 1])
        k_out = sb("k_out", [P, 1])
        gstat = sb("gstat", [P, 8, 2, 6])

        S = [ctx.enter_context(nc.psum_tensor(f"S{m}", [P, 2, BANK], F32)) for m in range(2)]
        TB = [ctx.enter_context(nc.psum_tensor(f"TB{m}", [P, BANK], F32)) for m in range(2)]
        PV = ctx.enter_context(nc.psum_tensor("PV", [P, BANK], F32))
        G = ctx.enter_context(nc.psum_tensor("G", [P, BANK], F32))

        def load_qkv(eng, done):
            src = wq.rearrange("(c p) (kv j n) -> c p kv j n", p=P, kv=KV, j=4)
            for c in range(DC):
                for pair in range(2):
                    for kv in range(2):
                        dst = wqkv[:, c, pair * BANK:(pair + 1) * BANK].rearrange("p (j kv n) -> p kv j n", j=4, kv=2)
                        eng.dma_start(dst[:, kv], src[c, :, 2 * pair + kv]).then_inc(done, 16)
            eng.dma_start(wqkv[:, :, QC:QC + KC], wk.rearrange("(c p) n -> p c n", p=P)).then_inc(done, 16)
            eng.dma_start(wqkv[:, :, QC + KC:QKV], wv.rearrange("(c p) n -> p c n", p=P)).then_inc(done, 16)
        N_CONST = 13
        N_QKV = 16 * (4 * DC + 2)

        s_wt = [sem(f"s_wt{w}") for w in range(3)]
        s_qkv = sem("s_qkv")
        s_small = sem("s_small")
        s_const = sem("s_const")
        s_abs = sem("s_abs")
        s_tot = sem("s_tot")
        s_totread = sem("s_totread")
        s_tern = sem("s_tern")
        s_ternT = sem("s_ternT")
        s_ternfree = sem("s_ternfree")
        s_lam = sem("s_lam")
        s_lamexp = sem("s_lamexp")
        s_dve0 = sem("s_dve0")
        with ExitStack() as once:
            wt = [sb(f"wt{w}", [P, EB * D], scope=once) for w in range(3)]
            isneg = sb("isneg", [P, 4096], F16, once)
            tern = [sb(f"tern{k}", [P, 4096], F16, once) for k in range(1)]
            ident_h = sb("ident_h", [P, P], F16, once)
            asum = sb("asum", [P, 3], scope=once)
            scale = sb("scale", [P, 3], scope=once)
            thr = sb("thr", [P, 3, 2], scope=once)
            kk = sb("kk", [P, 2], scope=once)
            lamv = sb("lamv", [P, 4, DH], scope=once)
            lamp = sb("lamp", [P, 2, DH], scope=once)
            lams = sb("lams", [P, 2], scope=once)
            lame = sb("lame", [P, 2], scope=once)
            block = once.enter_context(nc.Block())

            @block.sync
            def _(sp):
                for w, src in enumerate((w_up, w_gate)):
                    for half in range(2):
                        sp.dma_start(wt[w][:, half * 4096:(half + 1) * 4096].rearrange("p (e d) -> p e d", d=D),
                                     src.rearrange("(e p) d -> p e d", p=P)[:, half * 8:half * 8 + 8, :])\
                            .then_inc(s_wt[w], 16)
                for half in range(2):
                    sp.dma_start(wt[2][:, half * 4096:(half + 1) * 4096].rearrange("p (c e) -> p c e", e=E),
                                 w_down.rearrange("(c p) e -> p c e", p=P)[:, half * 2:half * 2 + 2, :])\
                        .then_inc(s_wt[2], 16)
                load_qkv(sp, s_qkv)
                sp.wait_ge(s_qkv, N_QKV)

            @block.gpsimd
            def _(pool):
                done = [0]

                def link(ins):
                    done[0] += 1
                    ins.then_inc(s_const, 1)
                    pool.wait_ge(s_const, done[0])

                for m in (ident, ident_b, ident_h, mask_b, blk64):
                    link(nc.gpsimd.memset(m[:, :], 0.0))
                link(nc.gpsimd.memset(ones[:, :], 1.0))
                link(nc.gpsimd.memset(mhalf[:, :], -0.5))
                link(nc.gpsimd.memset(blk64[0:64, 0:64], 1.0 / 64))
                link(nc.gpsimd.memset(blk64[64:128, 64:128], 1.0 / 64))
                for m in (ident, ident_b, ident_h):
                    link(nc.gpsimd.affine_select(out=m[:, :], in_=m[:, :], compare_op=ALU.not_equal, fill=1.0, base=0,
                                                 pattern=[[-1, P]], channel_multiplier=1))
                link(nc.gpsimd.affine_select(out=mask_b[:, :], in_=mask_b[:, :], compare_op=ALU.is_ge, fill=NEG,
                                             base=0, pattern=[[-1, P]], channel_multiplier=1))
                assert done[0] == N_CONST

            @block.scalar
            def _(act):
                for k, v in enumerate((lq1, lk1, lq2, lk2)):
                    act.dma_start(lamv[:, k, :], v.rearrange("(o n) -> o n", o=1).broadcast_to((P, DH)))\
                        .then_inc(s_small, 16)
                act.dma_start(rope_sb[:, :, :, :], rope.rearrange("(t p) f d -> p t f d", p=P)).then_inc(s_small, 16)
                for dst, src in ((gnw_sb, gn_w), (gnb_sb, gn_b)):
                    v = src.rearrange("(pair kv j d o) -> kv d pair j o", pair=2, kv=2, j=4, o=1)
                    for kv in range(2):
                        for pair in range(2):
                            act.dma_start(dst[64 * kv:64 * kv + 64, 4 * pair:4 * pair + 4]
                                          .rearrange("d (j o) -> d j o", o=1), v[kv, :, pair],
                                          allow_slow_non_contiguous=True).then_inc(s_small, 16)
                act.wait_ge(s_lam, 1)
                nc.scalar.activation(lame[:, :], lams[:, :], ACT.Exp).then_inc(s_lamexp, 1)
                for w in range(3):
                    for half in range(2):
                        for b in range(4):
                            n = 8 * w + 4 * half + b
                            act.wait_ge(s_ternT, n + 1)
                            src = TB[n % 2][:, :].bitcast(F16)
                            if w < 2:
                                dst = (up_t, gate_t)[w][:, b, half * 1024:(half + 1) * 1024]
                            else:
                                dst = down_t[:, 4 * b:4 * b + 4, half * 256:(half + 1) * 256]
                                src = src.rearrange("p (e d) -> p e d", e=4)
                            nc.scalar.activation(dst, src, ACT.Copy, saturate=False).then_inc(s_ternfree, 1)

            @block.vector
            def _(dve):
                chain = [0]

                def link(ins):
                    chain[0] += 1
                    ins.then_inc(s_dve0, 1)
                    dve.wait_ge(s_dve0, chain[0])

                dve.wait_ge(s_small, 16 * 13)
                lv = lamv[:, :, :].rearrange("p (a b) d -> p a b d", b=2)
                link(nc.vector.tensor_tensor(lamp[:, :, :], lv[:, :, 0, :], lv[:, :, 1, :], ALU.mult))
                nc.vector.tensor_reduce(lams[:, :], lamp[:, :, :], AX.X, ALU.add).then_inc(s_lam, 1)
                dve.wait_ge(s_lamexp, 1)
                nc.vector.scalar_tensor_tensor(neglam[:, :], lame[:, 1:2], -LAMBDA_INIT, lame[:, 0:1],
                                               ALU.add, ALU.subtract)
                for w in range(3):
                    dve.wait_ge(s_wt[w], 32)
                    nc.vector.tensor_reduce(asum[:, w:w + 1], wt[w][:, :], AX.X, ALU.add,
                                            apply_absolute_value=True).then_inc(s_abs, 1)
                    dve.wait_ge(s_tot, w + 1)
                    link(nc.vector.tensor_scalar(scale[:, w:w + 1], PV[:, w:w + 1], 1.0 / (E * D), TERNARY_EPS,
                                                 ALU.mult, ALU.add))
                    nc.vector.tensor_scalar(thr[:, w, 0:1], scale[:, w:w + 1], 0.5, None, ALU.mult)
                    link(nc.vector.tensor_scalar(thr[:, w, 1:2], scale[:, w:w + 1], -0.5, None, ALU.mult))
                    for half in range(2):
                        n = 2 * w + half
                        src = wt[w][:, half * 4096:(half + 1) * 4096]
                        link(nc.vector.tensor_scalar(isneg[:, :], src, thr[:, w, 1:2], None, ALU.is_lt))
                        if n >= 1:
                            dve.wait_ge(s_ternT, 4 * n)
                        nc.vector.scalar_tensor_tensor(tern[0][:, :], src, thr[:, w, 0:1], isneg[:, :],
                                                       ALU.is_gt, ALU.subtract).then_inc(s_tern, 1)
                        dve.wait_ge(s_tern, n + 1)
                nc.vector.tensor_scalar(k_silu[:, :], scale[:, 0:1], 1.0 / XS, None, ALU.mult)
                link(nc.vector.tensor_scalar(kk[:, 0:1], scale[:, 0:1], XS * HS, None, ALU.mult))
                nc.vector.reciprocal(k_hid[:, :], kk[:, 0:1])
                link(nc.vector.tensor_scalar(kk[:, 1:2], scale[:, 0:1], scale[:, 1:2], HS, ALU.mult, ALU.mult))
                link(nc.vector.tensor_scalar(k_out[:, :], kk[:, 1:2], scale[:, 2:3], None, ALU.mult))

            @block.tensor
            def _(pe):
                pe.wait_ge(s_const, N_CONST)
                for w in range(3):
                    pe.wait_ge(s_abs, w + 1)
                    if w:
                        pe.wait_ge(s_tern, 2 * w)
                    nc.tensor.matmul(PV[:, w:w + 1], ones[:, :], asum[:, w:w + 1], start=True, stop=True)\
                        .then_inc(s_tot, 1)
                    for half in range(2):
                        pe.wait_ge(s_tern, 2 * w + half + 1)
                        for b in range(4):
                            n = 8 * w + 4 * half + b
                            if n >= 2:
                                pe.wait_ge(s_ternfree, n - 1)
                            bank = TB[n % 2][:, :].bitcast(F16)
                            for k in range(8):
                                if w < 2:
                                    at = k * D + b * P
                                else:
                                    at = (k % 2) * E + (4 * b + k // 2) * P
                                last = nc.tensor.transpose(bank[:, k * P:(k + 1) * P], tern[0][:, at:at + P],
                                                           ident_h[:, :])
                            last.then_inc(s_ternT, 1)

        s_xin = [sem(f"s_xin{k}") for k in range(2)]
        s_wo = sem("s_wo")
        s_tfull = sem("s_tfull")
        s_tfree = sem("s_tfree")
        s_gfull = sem("s_gfull")
        s_gfree = sem("s_gfree")
        s_hi = sem("s_hi")
        s_hl = sem("s_hl")
        s_score = sem("s_score")
        s_negmax = sem("s_negmax")
        s_exp = sem("s_exp")
        s_comb = sem("s_comb")
        s_rot = sem("s_rot")
        s_linv = sem("s_linv")
        s_pv = sem("s_pv")
        s_pvfree = sem("s_pvfree")
        s_rcopy = sem("s_rcopy")
        s_dve = sem("s_dve")
        s_xr = [sem(f"s_xr{k}") for k in range(4)]
        s_gst = sem("s_gst")
        s_mv = sem("s_mv")
        s_gm = sem("s_gm")
        s_gv = sem("s_gv")
        s_gvm = sem("s_gvm")
        s_gr = sem("s_gr")
        s_grs = sem("s_grs")
        s_aff = sem("s_aff")
        s_nv = sem("s_nv")
        s_na = sem("s_na")
        s_y = sem("s_y")
        s_yfree = sem("s_yfree")
        s_var = sem("s_var")
        s_eps = sem("s_eps")
        s_rstd = sem("s_rstd")
        s_x1 = sem("s_x1")
        s_x1T = sem("s_x1T")
        s_xhi = sem("s_xhi")
        s_xlo = sem("s_xlo")
        s_ug = sem("s_ug")
        s_sl = sem("s_sl")
        s_h = sem("s_h")
        s_hhi = sem("s_hhi")
        s_hlo = sem("s_hlo")
        s_ready = sem("s_ready")
        s_od = [sem(f"s_od{k}") for k in range(2)]
        s_qkv2 = sem("s_qkv2")
        s_dve2 = sem("s_dve2")
        round_sems = sems[sems.index(s_xin[0]):]

        with nc.Fori(0, B) as b:
            with ExitStack() as att:
                xt = sb("xt", [P, 2, D], scope=att)
                x_t = sb("x_t", [P, DC, P], scope=att)
                t1 = sb("t1", [P, BANK], scope=att)
                t2 = sb("t2", [P, BANK], scope=att)
                hl = sb("hl", [P, 24, 4, DH], scope=att)
                qstk = sb("qstk", [P, 32, P], F32R, att)
                kstk = sb("kstk", [P, 8, T], F32R, att)
                v_sb = sb("v_sb", [P, NT, KC], scope=att)
                e1 = [sb(f"e1_{k}", [P, T], scope=att) for k in range(3)]
                e2 = [sb(f"e2_{k}", [P, T], scope=att) for k in range(2)]
                nmax = sb("nmax", [P, 8], scope=att)
                lsum = sb("lsum", [P, 2, 2], scope=att)
                linv = sb("linv", [P, 8, 2], scope=att)
                coef = sb("coef", [P, 2], scope=att)
                dt_sb = sb("dt_sb", [P, NT, 4, P], scope=att)
                r_sb = sb("r_sb", [P, P], scope=att)
                block = att.enter_context(nc.Block())

                def halves(t):
                    w = (t + 1) * P
                    return (1, w) if w <= BANK else (2, w // 2)

                def score_slot(n, m):
                    u = 2 * n + m
                    parts, w = halves(n // H)
                    if parts == 1:
                        return S[u % 2][:, u // 2 % 2:u // 2 % 2 + 1, 0:w], u - 3
                    return S[u % 2][:, :, 0:w], u - 1

                @block.sync
                def _(sp):
                    for t in range(NT):
                        if t >= 2:
                            sp.wait_ge(s_tfull, T_INDEX["x", t - 2, 0] + 1)
                        sp.dma_start(xt[:, t % 2, :], x_tiles[bass.ds(b, 1), t].rearrange("o p d -> p (o d)"))\
                            .then_inc(s_xin[t % 2], 16)
                    sp.wait_ge(s_gfree, 3 * NT)
                    wo_v = wo.rearrange("(pair kv j d) n -> kv d pair j n", pair=2, kv=2, j=4)
                    for kv in range(2):
                        for pair in range(2):
                            sp.dma_start(wo_sb[64 * kv:64 * kv + 64, 4 * pair:4 * pair + 4, :], wo_v[kv, :, pair])\
                                .then_inc(s_wo, 16)
                    sp.wait_ge(s_wo, 64)

                @block.tensor
                def _(pe):
                    def t_bank(use):
                        n = T_INDEX[use]
                        if n >= 2:
                            pe.wait_ge(s_tfree, n - 1)
                        return TB[n % 2]

                    def fill(use):
                        kind = use[0]
                        if kind == "x":
                            t = use[1]
                            pe.wait_ge(s_xin[t % 2], 16 * (t // 2 + 1))
                            bank = t_bank(use)
                            for c in range(DC):
                                last = nc.tensor.transpose(bank[:, c * P:(c + 1) * P],
                                                           xt[:, t % 2, c * P:(c + 1) * P], ident[:, :])
                        elif kind in "qk":
                            _, t, k = use
                            chunk = 2 if kind == "k" else k // 4
                            pe.wait_ge(s_hl, g_index(t, chunk) + 1)
                            bank = t_bank(use)
                            for m in range(4):
                                row = 16 + 4 * k + m if kind == "k" else 4 * (k % 4) + m
                                last = nc.tensor.transpose(bank[:, m * P:(m + 1) * P],
                                                           hl[:, row, :, :].rearrange("p a d -> p (a d)"), ident[:, :])
                        else:
                            _, n, half = use
                            pe.wait_ge(s_comb, n + 1)
                            bank = t_bank(use)
                            for k in range(min(4, n // H + 1 - 4 * half)):
                                at = (4 * half + k) * P
                                last = nc.tensor.transpose(bank[:, k * P:(k + 1) * P], e1[n % 3][:, at:at + P],
                                                           ident[:, :])
                        last.then_inc(s_tfull, 1)

                    def project(t, chunk, c):
                        g = g_index(t, chunk)
                        if c == 0:
                            pe.wait_ge(s_tfree, T_INDEX["x", t, 0] + 1)
                            if g:
                                pe.wait_ge(s_gfree, g)
                        last = nc.tensor.matmul(G[:, :], x_t[:, c, :], wqkv[:, c, chunk * BANK:(chunk + 1) * BANK],
                                                start=c == 0, stop=c == DC - 1)
                        if c == DC - 1:
                            last.then_inc(s_gfull, 1)

                    def scores(n, m):
                        t, i = divmod(n, H)
                        _, kv, _ = head_of(i)
                        parts, w = halves(t)
                        slot, used = score_slot(n, m)
                        pe.wait_ge(s_tfree, T_INDEX["q", t, i // 2] + 1)
                        pe.wait_ge(s_tfree, T_INDEX["k", t, kv // 2] + 1)
                        if used > 0:
                            pe.wait_ge(s_exp, used)
                        for h in range(parts):
                            nc.tensor.matmul(slot[:, h, :], qstk[:, 2 * i + m, :],
                                             kstk[:, 2 * kv + m, h * w:(h + 1) * w], start=True, stop=h < parts - 1)
                        nc.tensor.matmul(slot[:, parts - 1, w - P:w], ident_b[:, :], mask_b[:, :],
                                         start=False, stop=True).then_inc(s_score, 1)

                    def values(duo, half):
                        t, i = divmod(2 * duo, H)
                        pair = head_of(i)[0]
                        blocks = range((t + 2) // 2) if half == 0 else range((t + 2) // 2, t + 1)
                        if half == 0:
                            pe.wait_ge(s_gfree, g_index(t, 2) + 1)
                            pe.wait_ge(s_tfree, T_INDEX["d", 2 * duo + 1, t // 4] + 1)
                            if duo:
                                pe.wait_ge(s_pvfree, duo)
                        for kb in blocks:
                            for kv in range(2):
                                at = (2 * pair + kv) * 2 * DH
                                last = nc.tensor.matmul(PV[64 * kv:64 * kv + 64, 0:P], v_sb[:, kb, at:at + 2 * DH],
                                                        dt_sb[:, kb, (2 * duo + kv) % 4, :],
                                                        start=kb == 0, stop=kb == t)
                        if half == 1:
                            pe.wait_ge(s_linv, 2 * duo + 2)
                            for kv in range(2):
                                n = 2 * duo + kv
                                last = nc.tensor.matmul(PV[64 * kv:64 * kv + 64, P:2 * P],
                                                        linv[:, n % 8, 0:1].broadcast_to((P, 2 * DH)), ident[:, :],
                                                        start=True, stop=True)
                            last.then_inc(s_pv, 1)

                    fill(("x", 0, 0))
                    for chunk in CHUNKS[:2]:
                        for c in range(DC):
                            project(0, chunk, c)
                    for use in T_FIRST[1:7]:
                        fill(use)
                    for c in range(DC):
                        project(0, CHUNKS[2], c)
                    for use in T_FIRST[7:]:
                        fill(use)
                    for step in range(STEPS):
                        for m in range(2):
                            if step < NH:
                                scores(step, m)
                            for use in t_uses(step, m):
                                fill(use)
                            t, i = divmod(step, H)
                            if m == 0 and t + 1 < NT and i in PROJECT_STEP:
                                project(t + 1, *PROJECT_STEP[i])
                        if step >= 4 and (step - 4) // 2 < DUOS:
                            values(*divmod(step - 4, 2))

                @block.scalar
                def _(act):
                    def copy_out(use):
                        n = T_INDEX[use]
                        kind = use[0]
                        src = TB[n % 2]
                        act.wait_ge(s_tfull, n + 1)
                        if kind == "x":
                            t = use[1]
                            if t:
                                act.wait_ge(s_gfull, 3 * t)
                            dst = x_t[:, :, :]
                            src = src[:, :].rearrange("p (c q) -> p c q", c=DC)
                        elif kind == "q":
                            k = use[2]
                            dst = qstk[:, 4 * k:4 * k + 4, :]
                            src = src[:, :].rearrange("p (m q) -> p m q", m=4)
                        elif kind == "k":
                            _, t, k = use
                            dst = kstk[:, 4 * k:4 * k + 4, t * P:(t + 1) * P]
                            src = src[:, :].rearrange("p (m q) -> p m q", m=4)
                        else:
                            _, n, half = use
                            blocks = min(4, n // H + 1 - 4 * half)
                            if n >= 4:
                                act.wait_ge(s_pv, n // 2 - 1)
                            dst = dt_sb[:, 4 * half:4 * half + blocks, n % 4, :]
                            src = src[:, 0:blocks * P].rearrange("p (k q) -> p k q", q=P)
                        nc.scalar.activation(dst, src, ACT.Copy).then_inc(s_tfree, 1)

                    for use in T_FIRST:
                        copy_out(use)
                    for n in range(STEPS):
                        for m in range(2):
                            for use in t_uses(n, m):
                                copy_out(use)
                            if n >= NH:
                                continue
                            parts, w = halves(n // H)
                            act.wait_ge(s_negmax, 2 * n + m + 1)
                            if m == 0 and n >= 3:
                                act.wait_ge(s_tfull, T_INDEX["d", n - 3, (n - 3) // H // 4] + 1)
                            if n >= 2:
                                act.wait_ge(s_comb, n - 1)
                            e = (e1[n % 3], e2[n % 2])[m]
                            nc.scalar.activation(e[:, 0:parts * w].rearrange("p (h w) -> p h w", h=parts),
                                                 score_slot(n, m)[0], ACT.Exp,
                                                 bias=nmax[:, (2 * n + m) % 8:(2 * n + m) % 8 + 1], scale=1.0,
                                                 accum_out=lsum[:, n % 2, m:m + 1]).then_inc(s_exp, 1)

                @block.gpsimd
                def _(pool):
                    for g in range(3 * NT):
                        cols = 8 * DH if CHUNKS[g % 3] == 2 else BANK
                        pool.wait_ge(s_gfree, g + 1)
                        nc.gpsimd.tensor_tensor(t1[:, 0:cols], t1[:, 0:cols], t2[:, 0:cols], ALU.add)\
                            .then_inc(s_rot, 1)

                @block.vector
                def _(dve):
                    def rotate(t, chunk, part):
                        g = g_index(t, chunk)
                        maps = 8 if chunk == 2 else 16
                        at = 16 if chunk == 2 else 0
                        a, c = t1[:, 0:maps * DH], t2[:, 0:maps * DH]
                        rows = hl[:, at:at + maps, :, :]
                        hi, lo = ((rows[:, :, 0:4:2, :], rows[:, :, 1:4:2, :]) if chunk == 2 else
                                  (rows[:, :, 0:2, :], rows[:, :, 2:4, :]))
                        twice = a.rearrange("p (m o d) -> p m o d", o=1, d=DH).broadcast_to((P, maps, 2, DH))
                        if part == 0:
                            f = 2 if chunk == 2 else 0
                            cos = rope_sb[:, t, f:f + 1, :].broadcast_to((P, maps, DH))
                            sin = rope_sb[:, t, f + 1:f + 2, :].rearrange("p o (i s) -> p o i s", s=2)\
                                .broadcast_to((P, maps, DH // 2, 2))
                            if g:
                                dve.wait_ge(s_hl, g)
                            dve.wait_ge(s_gfull, g + 1)
                            if chunk == 2:
                                nc.vector.tensor_copy(v_sb[:, t, :], G[:, KC:2 * KC])
                            nc.vector.tensor_tensor(a.rearrange("p (m d) -> p m d", d=DH),
                                                    G[:, 0:maps * DH].rearrange("p (m d) -> p m d", d=DH), cos, ALU.mult)
                            nc.vector.tensor_tensor(
                                c.rearrange("p (m i s) -> p m i s", i=DH // 2, s=2),
                                G[:, 0:maps * DH].rearrange("p (m i s) -> p m i s", i=DH // 2, s=2)[:, :, :, ::-1],
                                sin, ALU.mult).then_inc(s_gfree, 1)
                        elif part == 1:
                            dve.wait_ge(s_rot, g + 1)
                            before = {0: ("q", t - 1, 7), 1: ("q", t, 3), 2: ("k", t - 1, 1)}[chunk]
                            if before in T_INDEX:
                                dve.wait_ge(s_tfull, T_INDEX[before] + 1)
                            nc.vector.tensor_scalar(hi.bitcast(I32), twice.bitcast(I32), HI_BITS, None,
                                                    ALU.bitwise_and).then_inc(s_hi, 1)
                        else:
                            dve.wait_ge(s_hi, g + 1)
                            nc.vector.tensor_tensor(lo, twice, hi, ALU.subtract).then_inc(s_hl, 1)

                    def neg_max(n, m):
                        u = 2 * n + m
                        dve.wait_ge(s_score, u + 1)
                        nc.vector.tensor_reduce(nmax[:, u % 8:u % 8 + 1], score_slot(n, m)[0], AX.XY, ALU.max,
                                                negate=True).then_inc(s_negmax, 1)

                    for chunk in CHUNKS:
                        for part in range(3):
                            rotate(0, chunk, part)
                    for step in range(STEPS):
                        n = step - 1
                        duo = (step - 6) // 2
                        done = step % 2 == 0 and 0 <= duo < DUOS
                        if done:
                            dve.wait_ge(s_pv, duo + 1)
                            nc.vector.tensor_copy(r_sb[:, :], PV[:, P:2 * P]).then_inc(s_rcopy, 1)
                        if step < NH:
                            neg_max(step, 0)
                        if done:
                            t, i = divmod(2 * duo, H)
                            pair, _, j = head_of(i)
                            dve.wait_ge(s_rcopy, duo + 1)
                            nc.vector.tensor_tensor(attn_t[:, pair, j, t * P:(t + 1) * P], PV[:, 0:P], r_sb[:, :],
                                                    ALU.mult).then_inc(s_pvfree, 1)
                        if 0 <= n < NH:
                            dve.wait_ge(s_exp, 2 * n + 2)
                            nc.vector.reciprocal(linv[:, n % 8, :], lsum[:, n % 2, :]).then_inc(s_linv, 1)
                        if step < NH:
                            neg_max(step, 1)
                        if 0 <= n < NH:
                            w = (n // H + 1) * P
                            dve.wait_ge(s_linv, n + 1)
                            nc.vector.tensor_scalar(coef[:, n % 2:n % 2 + 1], lsum[:, n % 2, 0:1], linv[:, n % 8, 1:2],
                                                    neglam[:, :], ALU.mult, ALU.mult).then_inc(s_dve, 1)
                            dve.wait_ge(s_dve, n + 1)
                            nc.vector.scalar_tensor_tensor(e1[n % 3][:, 0:w], e2[n % 2][:, 0:w],
                                                           coef[:, n % 2:n % 2 + 1], e1[n % 3][:, 0:w],
                                                           ALU.mult, ALU.add).then_inc(s_comb, 1)
                        t, i = divmod(step, H)
                        if 0 < t < NT and i in ROTATE_LATE:
                            rotate(t, *ROTATE_LATE[i])
                        if t + 1 < NT and i in ROTATE_STEP:
                            rotate(t + 1, *ROTATE_STEP[i])
                        if t == 4 and 6 <= i < 14:
                            if i == 6:
                                dve.wait_ge(s_pvfree, DUOS // 2)
                            j = i - 6
                            nc.vector.bn_stats(gstat[:, j, 0, :], attn_t[:, j // 4, j % 4, 0:T // 2])

            with ExitStack() as mix:
                x1 = sb("x1", [P, NT, D], scope=mix)
                x1_hi = sb("x1_hi", [P, DC, T], F16, mix)
                x1_lo = sb("x1_lo", [P, DC, T], F16, mix)
                hid_hi = sb("hid_hi", [P, EB, BANK], F16, mix)
                hid_lo = sb("hid_lo", [P, EB, BANK], F16, mix)
                sl = sb("sl", [P, 2, BANK], scope=mix)
                hh = sb("hh", [P, 2, BANK], scope=mix)
                z = sb("z", [P, 2, D], scope=mix)
                mv = sb("mv", [P, 8, 2], scope=mix)
                gm = sb("gm", [P, 8], scope=mix)
                dm = sb("dm", [P, 8], scope=mix)
                rv = sb("rv", [P, 8], scope=mix)
                gv = sb("gv", [P, 8], scope=mix)
                rs = sb("rs", [P, 8], scope=mix)
                fac = sb("fac", [P, 8], scope=mix)
                off = sb("off", [P, 8], scope=mix)
                lst = sb("lst", [P, 2, 6], scope=mix)
                lmv = sb("lmv", [P, 2, 2], scope=mix)
                lrs = sb("lrs", [P, 2], scope=mix)
                block = mix.enter_context(nc.Block())
                Y = [PV, G]
                NF = 2 * EB
                NY = 2 * NT

                @block.sync
                def _(sp):
                    for k in range(4):
                        sp.dma_start(x1[:, 2 * k:2 * k + 2, :],
                                     x_tiles[bass.ds(b, 1), 2 * k:2 * k + 2].rearrange("o t p d -> p (o t) d"))\
                            .then_inc(s_xr[k], 16)
                    sp.wait_ge(s_y, NT)
                    load_qkv(sp, s_qkv2)
                    for k in range(NT):
                        sp.wait_ge(s_ready, k + 1)
                        sp.dma_start(out_tiles[bass.ds(b, 1), k].rearrange("o p d -> p (o d)"), z[:, k % 2, :])\
                            .then_inc(s_od[k % 2], 16)
                    for k in range(2):
                        sp.wait_ge(s_od[k], 16 * (NT // 2))
                    sp.wait_ge(s_qkv2, N_QKV)

                @block.gpsimd
                def _(pool):
                    pool.wait_ge(s_gr, 1)
                    nc.gpsimd.tensor_scalar(gv[:, :], gv[:, :], LN_EPS, None, ALU.add).then_inc(s_eps, 1)
                    pool.wait_ge(s_eps, 1)
                    nc.gpsimd.tensor_tensor(rs[:, :], gv[:, :], mhalf[:, :], ALU.pow).then_inc(s_grs, 1)
                    for k in range(NY):
                        pool.wait_ge(s_var, k + 1)
                        veps = lmv[:, k % 2, 1:2]
                        nc.gpsimd.tensor_scalar(veps, veps, LN_EPS, None, ALU.add).then_inc(s_eps, 1)
                        pool.wait_ge(s_eps, k + 2)
                        nc.gpsimd.tensor_tensor(lrs[:, k % 2:k % 2 + 1], veps, mhalf[:, 0:1], ALU.pow)\
                            .then_inc(s_rstd, 1)

                @block.tensor
                def _(pe):
                    def x1_transposed(k):
                        pe.wait_ge(s_x1, k + 1)
                        if k >= 2:
                            pe.wait_ge(s_xlo, k - 1)
                        for c in range(DC):
                            last = nc.tensor.transpose(TB[k % 2][:, c * P:(c + 1) * P], x1[:, k, c * P:(c + 1) * P],
                                                       ident[:, :])
                        last.then_inc(s_x1T, 1)

                    def up_gate(f):
                        ch, eb = divmod(f, EB)
                        if f == 0:
                            pe.wait_ge(s_xlo, 4)
                        if f == EB:
                            pe.wait_ge(s_xlo, 8)
                        if f >= 2:
                            pe.wait_ge(s_h, f - 1)
                        for k, w in enumerate((up_t, gate_t)):
                            for c in range(DC):
                                for part in (x1_hi, x1_lo):
                                    last = nc.tensor.matmul(S[f % 2][:, k, :], w[:, c, eb * P:(eb + 1) * P],
                                                            part[:, c, ch * BANK:(ch + 1) * BANK],
                                                            start=c == 0 and part is x1_hi,
                                                            stop=c == DC - 1 and part is x1_lo)
                        last.then_inc(s_ug, 1)

                    pe.wait_ge(s_mv, 1)
                    nc.tensor.matmul(TB[0][:, 0:8], blk64[:, :], mv[:, :, 0], start=True, stop=True).then_inc(s_gm, 1)
                    pe.wait_ge(s_gv, 1)
                    nc.tensor.matmul(TB[1][:, 0:8], blk64[:, :], rv[:, :], start=True, stop=True).then_inc(s_gvm, 1)
                    for k in range(NT):
                        half = k // 4
                        pe.wait_ge(s_nv, 4 * half + 4)
                        pe.wait_ge(s_na, 4 * half + 4)
                        if k >= 2:
                            pe.wait_ge(s_yfree, k - 1)
                        for c in range(8):
                            last = nc.tensor.matmul(Y[k % 2][:, :], attn_t[:, c // 4, c % 4, k * P:(k + 1) * P],
                                                    wo_sb[:, c, :], start=c == 0, stop=c == 7)
                        last.then_inc(s_y, 1)
                        if k >= 2:
                            x1_transposed(k - 2)
                    up_gate(0)
                    x1_transposed(NT - 2)
                    x1_transposed(NT - 1)
                    for ch in range(2):
                        for eb in range(EB):
                            if ch or eb:
                                up_gate(ch * EB + eb)
                        for j in range(4):
                            y = NT + 4 * ch + j
                            pe.wait_ge(s_yfree, y - 1)
                            for eb in range(EB):
                                if j == 0:
                                    pe.wait_ge(s_hlo, ch * EB + eb + 1)
                                for part in (hid_hi, hid_lo):
                                    last = nc.tensor.matmul(Y[y % 2][:, :], part[:, eb, j * P:(j + 1) * P],
                                                            down_t[:, eb, :], start=eb == 0 and part is hid_hi,
                                                            stop=eb == EB - 1 and part is hid_lo)
                            last.then_inc(s_y, 1)

                @block.scalar
                def _(act):
                    def x1_high(k):
                        act.wait_ge(s_x1T, k + 1)
                        nc.scalar.activation(x1_hi[:, :, k * P:(k + 1) * P],
                                             TB[k % 2][:, :].rearrange("p (c q) -> p c q", c=DC),
                                             ACT.Copy, scale=XS).then_inc(s_xhi, 1)

                    def hidden_high(f):
                        act.wait_ge(s_h, f + 1)
                        if f >= EB and f % EB == 0:
                            act.wait_ge(s_y, NT + 4 * (f // EB))
                        nc.scalar.activation(hid_hi[:, f % EB, :], hh[:, f % 2, :], ACT.Copy).then_inc(s_hhi, 1)

                    act.wait_ge(s_aff, 1)
                    for half in range(2):
                        for j in range(4, 8):
                            v = attn_t[:, j // 4, j % 4, half * BANK:(half + 1) * BANK]
                            nc.scalar.activation(v, v, ACT.Identity, bias=off[:, j:j + 1], scale=fac[:, j:j + 1])\
                                .then_inc(s_na, 1)
                    for k in range(NT - 2):
                        x1_high(k)
                    for f in range(NF):
                        act.wait_ge(s_ug, f + 1)
                        if f >= 2:
                            act.wait_ge(s_h, f - 1)
                        nc.scalar.activation(sl[:, f % 2, :], S[f % 2][:, 0, :], ACT.Silu, scale=k_silu[:, :])\
                            .then_inc(s_sl, 1)
                        if f == 0:
                            x1_high(NT - 2)
                            x1_high(NT - 1)
                        if f % EB:
                            hidden_high(f - 1)
                        if f % EB == EB - 1:
                            hidden_high(f)

                @block.vector
                def _(dve):
                    chain = [0]

                    def link(ins):
                        chain[0] += 1
                        ins.then_inc(s_dve2, 1)
                        dve.wait_ge(s_dve2, chain[0])

                    def variance(k, v):
                        link(nc.vector.bn_stats(lst[:, k % 2, :], v))
                        nc.vector.bn_aggr(lmv[:, k % 2, :], lst[:, k % 2, :]).then_inc(s_var, 1)

                    def normalised(k, v):
                        dve.wait_ge(s_rstd, k + 1)
                        return nc.vector.tensor_scalar(v, v, lmv[:, k % 2, 0:1], lrs[:, k % 2:k % 2 + 1],
                                                       ALU.subtract, ALU.mult)

                    def x1_low(k):
                        dve.wait_ge(s_xhi, k + 1)
                        nc.vector.scalar_tensor_tensor(x1_lo[:, :, k * P:(k + 1) * P],
                                                       TB[k % 2][:, :].rearrange("p (c q) -> p c q", c=DC), XS,
                                                       x1_hi[:, :, k * P:(k + 1) * P], ALU.mult, ALU.subtract)\
                            .then_inc(s_xlo, 1)

                    def hidden_low(f):
                        dve.wait_ge(s_hhi, f + 1)
                        nc.vector.tensor_tensor(hid_lo[:, f % EB, :], hh[:, f % 2, :], hid_hi[:, f % EB, :],
                                                ALU.subtract).then_inc(s_hlo, 1)

                    for j in range(8):
                        last = nc.vector.bn_stats(gstat[:, j, 1, :], attn_t[:, j // 4, j % 4, T // 2:T])
                    last.then_inc(s_gst, 1)
                    dve.wait_ge(s_gst, 1)
                    for j in range(8):
                        last = nc.vector.bn_aggr(mv[:, j, :], gstat[:, j, :, :].rearrange("p h s -> p (h s)"))
                    last.then_inc(s_mv, 1)
                    dve.wait_ge(s_gm, 1)
                    nc.vector.tensor_copy(gm[:, :], TB[0][:, 0:8])
                    dve.wait_ge(s_mv, 1)
                    link(nc.vector.tensor_tensor(dm[:, :], mv[:, :, 0], TB[0][:, 0:8], ALU.subtract))
                    link(nc.vector.tensor_tensor(dm[:, :], dm[:, :], dm[:, :], ALU.mult))
                    nc.vector.tensor_tensor(rv[:, :], dm[:, :], mv[:, :, 1], ALU.add).then_inc(s_gv, 1)
                    dve.wait_ge(s_gvm, 1)
                    nc.vector.tensor_copy(gv[:, :], TB[1][:, 0:8]).then_inc(s_gr, 1)
                    dve.wait_ge(s_grs, 1)
                    link(nc.vector.tensor_tensor(fac[:, :], gnw_sb[:, :], rs[:, :], ALU.mult))
                    link(nc.vector.tensor_scalar(fac[:, :], fac[:, :], 1.0 - LAMBDA_INIT, None, ALU.mult))
                    link(nc.vector.tensor_tensor(dm[:, :], gm[:, :], fac[:, :], ALU.mult))
                    nc.vector.scalar_tensor_tensor(off[:, :], gnb_sb[:, :], 1.0 - LAMBDA_INIT, dm[:, :],
                                                   ALU.mult, ALU.subtract).then_inc(s_aff, 1)
                    dve.wait_ge(s_aff, 1)
                    for half in range(2):
                        for j in range(4):
                            v = attn_t[:, j // 4, j % 4, half * BANK:(half + 1) * BANK]
                            nc.vector.tensor_scalar(v, v, fac[:, j:j + 1], off[:, j:j + 1], ALU.mult, ALU.add)\
                                .then_inc(s_nv, 1)

                    for k in range(NT + 1):
                        if k < NT:
                            dve.wait_ge(s_xr[k // 2], 16)
                            dve.wait_ge(s_y, k + 1)
                            nc.vector.tensor_tensor(x1[:, k, :], Y[k % 2][:, :], x1[:, k, :], ALU.add)\
                                .then_inc(s_yfree, 1)
                            dve.wait_ge(s_yfree, k + 1)
                            variance(k, x1[:, k, :])
                        if k >= 1:
                            normalised(k - 1, x1[:, k - 1, :]).then_inc(s_x1, 1)
                        if k >= 3:
                            x1_low(k - 3)

                    for ch in range(2):
                        for eb in range(EB):
                            f = ch * EB + eb
                            dve.wait_ge(s_sl, f + 1)
                            if f >= 2:
                                dve.wait_ge(s_hhi, f - 1)
                                dve.wait_ge(s_hlo, f - 1)
                            nc.vector.scalar_tensor_tensor(hh[:, f % 2, :], sl[:, f % 2, :], k_hid[:, :],
                                                           S[f % 2][:, 1, :], ALU.mult, ALU.mult).then_inc(s_h, 1)
                            if f == 0:
                                x1_low(NT - 2)
                                x1_low(NT - 1)
                            if eb:
                                hidden_low(f - 1)
                        hidden_low(ch * EB + EB - 1)
                        for j in range(4):
                            k = 4 * ch + j
                            y = NT + k
                            v = z[:, k % 2, :]
                            dve.wait_ge(s_y, y + 1)
                            if k >= 2:
                                dve.wait_ge(s_od[k % 2], 16 * (k // 2))
                            nc.vector.scalar_tensor_tensor(v, Y[y % 2][:, :], k_out[:, :], x1[:, k, :],
                                                           ALU.mult, ALU.add).then_inc(s_yfree, 1)
                            dve.wait_ge(s_yfree, y + 1)
                            variance(y, v)
                            normalised(y, v).then_inc(s_ready, 1)

            nc.all_engine_barrier()
            for s in round_sems:
                nc.sync.sem_clear(s)
            nc.all_engine_barrier()


_INS = ["x", "Wq", "Wk", "Wv", "Wo", "lambda_q1", "lambda_k1", "lambda_q2", "lambda_k2", "gn_w", "gn_b"]


def rope_table():
    inv = (1.0 / np.float32(10000.0) ** (np.arange(0, DH, 2, dtype=np.float32) / np.float32(DH))).astype(np.float32)
    freqs = np.arange(T, dtype=np.float32)[:, None] * inv[None, :]
    cos = np.repeat(np.cos(freqs), 2, axis=1)
    sin = np.repeat(np.sin(freqs), 2, axis=1) * np.tile(np.array([-1.0, 1.0], np.float32), DH // 2)
    s = np.float32(1.0 / math.sqrt(DH))
    return np.ascontiguousarray(np.stack([cos * s, sin * s, cos, sin], axis=1).astype(np.float32))


def kernel(**inputs):
    import concourse.bacc as bacc
    from concourse.bass_utils import run_bass_kernel_spmd

    nc = bacc.Bacc("TRN2", target_bir_lowering=False, num_devices=1)
    named = [("L0_attn_" + n) for n in _INS] + ["L0_ffn_W_up", "L0_ffn_W_gate", "L0_ffn_W_down"]
    arrays = {f"in_{n}": np.ascontiguousarray(inputs[n]) for n in named}
    arrays["in_rope"] = rope_table()
    args = [nc.dram_tensor(n, a.shape, mybir.dt.from_np(a.dtype), kind="ExternalInput").ap() for n, a in arrays.items()]
    args.append(nc.dram_tensor("out", (B, T, D), F32, kind="ExternalOutput").ap())
    layer_kernel(nc, *args)
    r = run_bass_kernel_spmd(nc, [arrays], core_ids=[0])
    return r.results[0]["out"]
```

```python
import math
from contextlib import ExitStack

import numpy as np
import concourse.bass as bass
from concourse import mybir

F32, F32R, F16, BF16 = mybir.dt.float32, mybir.dt.float32r, mybir.dt.float16, mybir.dt.bfloat16
F8, I32 = mybir.dt.float8e4, mybir.dt.int32
ACT = mybir.ActivationFunctionType
ALU = mybir.AluOpType
AX = mybir.AxisListType

B, T, D = 4, 1024, 512
H, KV, DH = 16, 4, 32
E = 2048
P = 128
NT = T // P
DC = D // P
EB = E // P
QC = H * 2 * DH
KC = KV * 2 * DH
QKV = QC + 2 * KC
BANK = 512
NH = NT * H
DUOS = NH // 2
LAMBDA_INIT = 0.8 - 0.6 * math.exp(-0.3 * 0)
LN_EPS = 1e-5
TERNARY_EPS = 1e-8
NEG = -3.0e38
HI_BITS = -4096
XS = 1024.0
HS = 8.0


def head_of(i):
    duo, r = divmod(i, 2)
    pair, j = divmod(duo, 4)
    return pair, 2 * pair + r, j


PROJECT_STEP = {1 + c: (0, c) for c in range(4)} | {6 + c: (2, c) for c in range(4)} | \
    {11 + c: (1, c) for c in range(4)}
ROTATE_STEP = {5: (0, 0), 7: (0, 1), 8: (0, 2), 10: (2, 0), 11: (2, 1), 12: (2, 2), 15: (1, 0)}
ROTATE_LATE = {0: (1, 1), 1: (1, 2)}
TWICE_STEP, TWICE_LATE = {9: 0, 13: 2}, {2: 1}
PARTS_STEP = {0: ("x", 0), 10: ("q", 0), 11: ("q", 1), 12: ("q", 2), 13: ("q", 3), 14: ("k", 0), 15: ("k", 1)}
PARTS_LATE = {3: ("q", 4), 4: ("q", 5), 5: ("q", 6), 6: ("q", 7)}


def t_uses(step, m):
    out = []
    n = step - 2
    if 0 <= n < NH and 4 * m < n // H + 1:
        out.append(("d", n, m))
    if step < NH and m == 1:
        t, i = divmod(step, H)
        if i in PARTS_LATE:
            out.append((PARTS_LATE[i][0], t, PARTS_LATE[i][1]))
        if t + 1 < NT and i in PARTS_STEP:
            out.append((PARTS_STEP[i][0], t + 1, PARTS_STEP[i][1]))
    return out


T_FIRST = [("x", 0, 0)] + [("q", 0, k) for k in range(4)] + [("k", 0, k) for k in range(2)]
STEPS = NH + 6
T_INDEX = {use: n for n, use in enumerate(T_FIRST + [u for s in range(STEPS) for m in range(2) for u in t_uses(s, m)])}
CHUNKS = (0, 2, 1)


def g_index(t, chunk):
    return 3 * t + CHUNKS.index(chunk)


def layer_kernel(nc, x, w_qkv, wo, lams_in, gn, w_up, w_gate, w_down, rope, out):
    x_tiles = x.rearrange("(n p) d -> n p d", p=P)
    out_tiles = out.rearrange("b (t p) d -> b t p d", p=P)

    ctx = ExitStack()
    with ctx:
        def sb(name, shape, dt=F32, scope=ctx):
            return scope.enter_context(nc.sbuf_tensor(name, shape, dt))

        sems = []

        def sem(name):
            s = ctx.enter_context(nc.semaphore(name))
            sems.append(s)
            return s

        wbig = sb("wbig", [P, DC * QKV])
        wqkv = wbig[:, :].rearrange("p (c n) -> p c n", c=DC)
        wo_sb = wbig[:, 0:8 * D].rearrange("p (c n) -> p c n", c=8)
        up_t = sb("up_t", [P, DC, E], F8)
        gate_t = sb("gate_t", [P, DC, E], F8)
        down_t = sb("down_t", [P, EB, D], F8)
        attn_t = sb("attn_t", [P, 2, 4, T])
        rope_sb = sb("rope_sb", [P, NT, 4, DH])
        ident = sb("ident", [P, P])
        ident_b = sb("ident_b", [P, P], BF16)
        mask_b = sb("mask_b", [P, P], BF16)
        ones = sb("ones", [P, P])
        blk64 = sb("blk64", [P, P])
        gn_sb = sb("gn_sb", [P, 2, 8])
        neglam = sb("neglam", [P, 1])
        mhalf = sb("mhalf", [P, 8])
        k_silu = sb("k_silu", [P, 1])
        k_hid = sb("k_hid", [P, 1])
        k_out = sb("k_out", [P, 1])
        xt = sb("xt", [P, 2, D])
        z = sb("z", [P, 2, D])
        gstat = sb("gstat", [P, 8, 3, 6])

        S = [ctx.enter_context(nc.psum_tensor(f"S{m}", [P, 2, BANK], F32)) for m in range(2)]
        TB = [ctx.enter_context(nc.psum_tensor(f"TB{m}", [P, BANK], F32)) for m in range(2)]
        PV = ctx.enter_context(nc.psum_tensor("PV", [P, BANK], F32))
        G = ctx.enter_context(nc.psum_tensor("G", [P, BANK], F32))

        def load_qkv(eng, done):
            for c in range(DC):
                eng.dma_start(wqkv[:, c, :], w_qkv[c * P:(c + 1) * P, :]).then_inc(done, 16)

        N_CONST = 11
        N_QKV = 16 * DC

        def load_x(eng, n, k):
            eng.dma_start(xt[:, k, :], x_tiles[bass.ds(n, 1)].rearrange("o p d -> p (o d)")).then_inc(s_xin[k], 16)

        s_xin = [sem(f"s_xin{k}") for k in range(2)]
        s_od = [sem(f"s_od{k}") for k in range(2)]
        ROUND_IO = 16 * (NT // 2)

        s_wt = [sem(f"s_wt{w}") for w in range(3)]
        s_qkv = sem("s_qkv")
        s_lamin = sem("s_lamin")
        s_small = sem("s_small")
        s_const = sem("s_const")
        s_abs = sem("s_abs")
        s_tot = sem("s_tot")
        s_totread = sem("s_totread")
        s_neg = sem("s_neg")
        s_tern = sem("s_tern")
        s_lam = sem("s_lam")
        s_lamexp = sem("s_lamexp")
        s_dve0 = sem("s_dve0")
        with ExitStack() as once:
            wt = [sb(f"wt{w}", [P, EB * D], scope=once) for w in range(3)]
            isneg = sb("isneg", [P, 2, 4096], F16, once)
            absw = attn_t[:, :, :, :].rearrange("p a j t -> p (a j t)")
            asum = sb("asum", [P, 3, 2], scope=once)
            scale = sb("scale", [P, 3], scope=once)
            thr = sb("thr", [P, 3, 2], scope=once)
            kk = sb("kk", [P, 2], scope=once)
            lamv = sb("lamv", [P, 2, 2, DH], scope=once)
            lamp = sb("lamp", [P, 2, DH], scope=once)
            lams = sb("lams", [P, 2], scope=once)
            lame = sb("lame", [P, 2], scope=once)
            block = once.enter_context(nc.Block())

            @block.sync
            def _(sp):
                for w, src in enumerate((w_up, w_gate, w_down)):
                    v = src.rearrange("(c p) n -> p c n", p=P)
                    c = v.shape[1] // 2
                    for half in range(2):
                        sp.dma_start(wt[w][:, half * 4096:(half + 1) * 4096].rearrange("p (c n) -> p c n", c=c),
                                     v[:, half * c:(half + 1) * c, :]).then_inc(s_wt[w], 16)
                load_qkv(sp, s_qkv)
                for k in range(2):
                    load_x(sp, k, k)
                sp.wait_ge(s_qkv, N_QKV)

            @block.gpsimd
            def _(pool):
                done = [0]

                def link(ins):
                    done[0] += 1
                    ins.then_inc(s_const, 1)
                    pool.wait_ge(s_const, done[0])

                for k in range(2):
                    nc.gpsimd.memset(z[:, k, 0:1], 0.0).then_inc(s_od[k], 1)
                for m in (ident, ident_b, mask_b, blk64):
                    link(nc.gpsimd.memset(m[:, :], 0.0))
                link(nc.gpsimd.memset(ones[:, :], 1.0))
                link(nc.gpsimd.memset(mhalf[:, :], -0.5))
                link(nc.gpsimd.memset(blk64[0:64, 0:64], 1.0 / 64))
                link(nc.gpsimd.memset(blk64[64:128, 64:128], 1.0 / 64))
                for m in (ident, ident_b):
                    link(nc.gpsimd.affine_select(out=m[:, :], in_=m[:, :], compare_op=ALU.not_equal, fill=1.0, base=0,
                                                 pattern=[[-1, P]], channel_multiplier=1))
                link(nc.gpsimd.affine_select(out=mask_b[:, :], in_=mask_b[:, :], compare_op=ALU.is_ge, fill=NEG,
                                             base=0, pattern=[[-1, P]], channel_multiplier=1))
                assert done[0] == N_CONST

            @block.scalar
            def _(act):
                act.dma_start(lamv[:, :, :, :], lams_in.rearrange("(o a) b d -> o a b d", o=1)
                              .broadcast_to((P, 2, 2, DH))).then_inc(s_lamin, 16)
                act.dma_start(rope_sb[:, :, :, :], rope.rearrange("(t p) f d -> p t f d", p=P)).then_inc(s_small, 16)
                act.dma_start(gn_sb[:, :, :], gn).then_inc(s_small, 16)
                act.wait_ge(s_lam, 1)
                nc.scalar.activation(lame[:, :], lams[:, :], ACT.Exp).then_inc(s_lamexp, 1)
                for w in range(3):
                    act.wait_ge(s_wt[w], 32)
                    for half in range(2):
                        if w:
                            act.wait_ge(s_abs, 2 * w - 1 + half)
                        cols = slice(half * 4096, (half + 1) * 4096)
                        nc.scalar.activation(absw[:, cols], wt[w][:, cols], ACT.Abs,
                                             accum_out=asum[:, w, half:half + 1]).then_inc(s_abs, 1)
                act.wait_ge(s_small, 32)

            @block.vector
            def _(dve):
                chain = [0]

                def link(ins):
                    chain[0] += 1
                    ins.then_inc(s_dve0, 1)
                    dve.wait_ge(s_dve0, chain[0])

                dve.wait_ge(s_lamin, 16)
                link(nc.vector.tensor_tensor(lamp[:, :, :], lamv[:, :, 0, :], lamv[:, :, 1, :], ALU.mult))
                nc.vector.tensor_reduce(lams[:, :], lamp[:, :, :], AX.X, ALU.add).then_inc(s_lam, 1)
                dve.wait_ge(s_lamexp, 1)
                nc.vector.scalar_tensor_tensor(neglam[:, :], lame[:, 1:2], -LAMBDA_INIT, lame[:, 0:1],
                                               ALU.add, ALU.subtract)
                for w, dst in enumerate((up_t, gate_t, down_t)):
                    dst = dst[:, :, :].rearrange("p c n -> p (c n)")
                    dve.wait_ge(s_tot, w + 1)
                    link(nc.vector.tensor_scalar(scale[:, w:w + 1], PV[:, w:w + 1], 1.0 / (E * D), TERNARY_EPS,
                                                 ALU.mult, ALU.add))
                    nc.vector.tensor_scalar(thr[:, w, 0:1], scale[:, w:w + 1], 0.5, None, ALU.mult)
                    nc.vector.tensor_scalar(thr[:, w, 1:2], scale[:, w:w + 1], -0.5, None, ALU.mult)\
                        .then_inc(s_totread, 1)
                    dve.wait_ge(s_totread, w + 1)
                    for half in range(2):
                        cols = slice(half * 4096, (half + 1) * 4096)
                        n = 2 * w + half
                        if n >= 2:
                            dve.wait_ge(s_tern, n - 1)
                        nc.vector.tensor_scalar(isneg[:, half, :], wt[w][:, cols], thr[:, w, 1:2], None, ALU.is_lt)\
                            .then_inc(s_neg, 1)
                        dve.wait_ge(s_neg, n + 1)
                        nc.vector.scalar_tensor_tensor(dst[:, cols], wt[w][:, cols], thr[:, w, 0:1], isneg[:, half, :],
                                                       ALU.is_gt, ALU.subtract, saturate=False).then_inc(s_tern, 1)
                nc.vector.tensor_scalar(k_silu[:, :], scale[:, 0:1], 1.0 / XS, None, ALU.mult)
                link(nc.vector.tensor_scalar(kk[:, 0:1], scale[:, 0:1], XS * HS, None, ALU.mult))
                nc.vector.reciprocal(k_hid[:, :], kk[:, 0:1])
                link(nc.vector.tensor_scalar(kk[:, 1:2], scale[:, 0:1], scale[:, 1:2], HS, ALU.mult, ALU.mult))
                link(nc.vector.tensor_scalar(k_out[:, :], kk[:, 1:2], scale[:, 2:3], None, ALU.mult))

            @block.tensor
            def _(pe):
                pe.wait_ge(s_const, N_CONST)
                for w in range(3):
                    pe.wait_ge(s_abs, 2 * w + 2)
                    if w:
                        pe.wait_ge(s_totread, w)
                    for half in range(2):
                        last = nc.tensor.matmul(PV[:, w:w + 1], ones[:, :], asum[:, w, half:half + 1],
                                                start=half == 0, stop=half == 1)
                    last.then_inc(s_tot, 1)

        s_wo = sem("s_wo")
        s_tfull = sem("s_tfull")
        s_tfree = sem("s_tfree")
        s_gfull = sem("s_gfull")
        s_gfree = sem("s_gfree")
        s_hi = sem("s_hi")
        s_lo = sem("s_lo")
        s_hl = sem("s_hl")
        s_score = sem("s_score")
        s_negmax = sem("s_negmax")
        s_exp = sem("s_exp")
        s_comb = sem("s_comb")
        s_rot = sem("s_rot")
        s_linv = sem("s_linv")
        s_pv = sem("s_pv")
        s_pvfree = sem("s_pvfree")
        s_rcopy = sem("s_rcopy")
        s_coef = sem("s_coef")
        s_xr = [sem(f"s_xr{k}") for k in range(4)]
        s_gst = sem("s_gst")
        s_mv = sem("s_mv")
        s_gm = sem("s_gm")
        s_gv = sem("s_gv")
        s_gvm = sem("s_gvm")
        s_gr = sem("s_gr")
        s_grs = sem("s_grs")
        s_aff = sem("s_aff")
        s_nv = sem("s_nv")
        s_na = sem("s_na")
        s_y = sem("s_y")
        s_yfree = sem("s_yfree")
        s_var = sem("s_var")
        s_eps = sem("s_eps")
        s_rstd = sem("s_rstd")
        s_x1 = sem("s_x1")
        s_x1T = sem("s_x1T")
        s_xhi = sem("s_xhi")
        s_xlo = sem("s_xlo")
        s_ug = sem("s_ug")
        s_sl = sem("s_sl")
        s_h = sem("s_h")
        s_hhi = sem("s_hhi")
        s_hlo = sem("s_hlo")
        s_ready = sem("s_ready")
        s_qkv2 = sem("s_qkv2")
        s_dve2 = sem("s_dve2")
        att_sems = sems[sems.index(s_wo):sems.index(s_xr[0])]
        mix_sems = sems[sems.index(s_xr[0]):]

        with nc.Fori(0, B) as b:
            with ExitStack() as att:
                x_t = sb("x_t", [P, DC, P], scope=att)
                t1 = sb("t1", [P, BANK], scope=att)
                t2 = sb("t2", [P, BANK], scope=att)
                hl = sb("hl", [P, 24, 4, DH], scope=att)
                qstk = sb("qstk", [P, 32, P], F32R, att)
                kstk = sb("kstk", [P, 8, T], F32R, att)
                v_sb = sb("v_sb", [P, NT, KC], scope=att)
                e1 = [sb(f"e1_{k}", [P, T], scope=att) for k in range(3)]
                e2 = [sb(f"e2_{k}", [P, T], scope=att) for k in range(2)]
                nmax = sb("nmax", [P, 8], scope=att)
                lsum = sb("lsum", [P, 2, 2], scope=att)
                linv = sb("linv", [P, 8, 2], scope=att)
                coef = sb("coef", [P, 2], scope=att)
                dt_sb = sb("dt_sb", [P, NT, 4, P], scope=att)
                r_sb = sb("r_sb", [P, P], scope=att)
                block = att.enter_context(nc.Block())

                EARLY = BANK // P * H

                ADD = BANK // 2

                def pieces(chunk):
                    return (KC if chunk == 2 else BANK) // ADD

                def g_bank(g):
                    return PV if g == 1 else G

                def halves(t):
                    w = (t + 1) * P
                    return (1, w) if w <= BANK else (2, w // 2)

                def score_slot(n, m):
                    u = 2 * n + m
                    parts, w = halves(n // H)
                    if parts == 1:
                        return S[u % 2][:, u // 2 % 2:u // 2 % 2 + 1, 0:w], u - 3
                    return S[u % 2][:, :, 0:w], u - 1

                @block.sync
                def _(sp):
                    for s in mix_sems:
                        sp.sem_clear(s)
                    for t in range(2, NT):
                        sp.wait_ge(s_tfull, T_INDEX["x", t - 2, 0] + 1)
                        load_x(sp, b * NT + t, t % 2)
                    sp.wait_ge(s_gfree, 3 * NT)
                    sp.dma_start(wo_sb, wo.rearrange("(c p) n -> p c n", p=P)).then_inc(s_wo, 16)
                    sp.wait_ge(s_wo, 16)

                @block.tensor
                def _(pe):
                    def t_bank(use):
                        n = T_INDEX[use]
                        if n >= 2:
                            pe.wait_ge(s_tfree, n - 1)
                        return TB[n % 2]

                    def fill(use):
                        kind = use[0]
                        if kind == "x":
                            t = use[1]
                            pe.wait_ge(s_xin[t % 2], b * ROUND_IO + 16 * (t // 2 + 1))
                            bank = t_bank(use)
                            for c in range(DC):
                                last = nc.tensor.transpose(bank[:, c * P:(c + 1) * P],
                                                           xt[:, t % 2, c * P:(c + 1) * P], ident[:, :])
                        elif kind in "qk":
                            _, t, k = use
                            chunk = 2 if kind == "k" else k // 4
                            pe.wait_ge(s_hl, g_index(t, chunk) + 1)
                            bank = t_bank(use)
                            for m in range(4):
                                row = 16 + 4 * k + m if kind == "k" else 4 * (k % 4) + m
                                last = nc.tensor.transpose(bank[:, m * P:(m + 1) * P],
                                                           hl[:, row, :, :].rearrange("p a d -> p (a d)"), ident[:, :])
                        else:
                            _, n, half = use
                            pe.wait_ge(s_comb, n + 1)
                            bank = t_bank(use)
                            for k in range(min(4, n // H + 1 - 4 * half)):
                                at = (4 * half + k) * P
                                last = nc.tensor.transpose(bank[:, k * P:(k + 1) * P], e1[n % 3][:, at:at + P],
                                                           ident[:, :])
                        last.then_inc(s_tfull, 1)

                    def project(t, chunk, c):
                        g = g_index(t, chunk)
                        if c == 0:
                            pe.wait_ge(s_tfree, T_INDEX["x", t, 0] + 1)
                            if g >= 2:
                                pe.wait_ge(s_gfree, g if g > 2 else 1)
                        last = nc.tensor.matmul(g_bank(g)[:, :], x_t[:, c, :], wqkv[:, c, chunk * BANK:(chunk + 1) * BANK],
                                                start=c == 0, stop=c == DC - 1)
                        if c == DC - 1:
                            last.then_inc(s_gfull, 1)

                    def scores(n, m):
                        t, i = divmod(n, H)
                        _, kv, _ = head_of(i)
                        parts, w = halves(t)
                        slot, used = score_slot(n, m)
                        pe.wait_ge(s_tfree, T_INDEX["q", t, i // 2] + 1)
                        pe.wait_ge(s_tfree, T_INDEX["k", t, kv // 2] + 1)
                        if used > 0:
                            pe.wait_ge(s_exp, used)
                        for h in range(parts):
                            nc.tensor.matmul(slot[:, h, :], qstk[:, 2 * i + m, :],
                                             kstk[:, 2 * kv + m, h * w:(h + 1) * w], start=True, stop=h < parts - 1)
                        nc.tensor.matmul(slot[:, parts - 1, w - P:w], ident_b[:, :], mask_b[:, :],
                                         start=False, stop=True).then_inc(s_score, 1)

                    def values(duo, half):
                        t, i = divmod(2 * duo, H)
                        pair = head_of(i)[0]
                        blocks = range((t + 2) // 2) if half == 0 else range((t + 2) // 2, t + 1)
                        if half == 0:
                            pe.wait_ge(s_gfree, g_index(t, 2) + 1)
                            pe.wait_ge(s_tfree, T_INDEX["d", 2 * duo + 1, t // 4] + 1)
                            if duo:
                                pe.wait_ge(s_pvfree, duo)
                        for kb in blocks:
                            for kv in range(2):
                                at = (2 * pair + kv) * 2 * DH
                                last = nc.tensor.matmul(PV[64 * kv:64 * kv + 64, 0:P], v_sb[:, kb, at:at + 2 * DH],
                                                        dt_sb[:, kb, (2 * duo + kv) % 4, :],
                                                        start=kb == 0, stop=kb == t)
                        if half == 1:
                            pe.wait_ge(s_linv, 2 * duo + 2)
                            for kv in range(2):
                                n = 2 * duo + kv
                                last = nc.tensor.matmul(PV[64 * kv:64 * kv + 64, P:2 * P],
                                                        linv[:, n % 8, 0:1].broadcast_to((P, 2 * DH)), ident[:, :],
                                                        start=True, stop=True)
                            last.then_inc(s_pv, 1)

                    fill(("x", 0, 0))
                    for chunk in CHUNKS:
                        for c in range(DC):
                            project(0, chunk, c)
                    for use in T_FIRST[1:]:
                        fill(use)
                    def project_piece(step):
                        t, i = divmod(step, H)
                        if t + 1 < NT and i in PROJECT_STEP:
                            project(t + 1, *PROJECT_STEP[i])

                    def values_half(step):
                        if step >= 4 and (step - 4) // 2 < DUOS:
                            values(*divmod(step - 4, 2))

                    for m in range(2):
                        scores(0, m)
                    for step in range(STEPS):
                        if step + 1 < EARLY:
                            for m in range(2):
                                scores(step + 1, m)
                                for use in t_uses(step, m):
                                    fill(use)
                            project_piece(step)
                            values_half(step)
                        else:
                            for use in t_uses(step, 0):
                                fill(use)
                            if EARLY <= step < NH:
                                scores(step, 1)
                            project_piece(step)
                            for use in t_uses(step, 1):
                                fill(use)
                            values_half(step)
                            if step + 1 < NH:
                                scores(step + 1, 0)

                @block.scalar
                def _(act):
                    def copy_out(use):
                        n = T_INDEX[use]
                        kind = use[0]
                        src = TB[n % 2]
                        act.wait_ge(s_tfull, n + 1)
                        if kind == "x":
                            t = use[1]
                            if t:
                                act.wait_ge(s_gfull, 3 * t)
                            dst = x_t[:, :, :]
                            src = src[:, :].rearrange("p (c q) -> p c q", c=DC)
                        elif kind == "q":
                            k = use[2]
                            dst = qstk[:, 4 * k:4 * k + 4, :]
                            src = src[:, :].rearrange("p (m q) -> p m q", m=4)
                        elif kind == "k":
                            _, t, k = use
                            dst = kstk[:, 4 * k:4 * k + 4, t * P:(t + 1) * P]
                            src = src[:, :].rearrange("p (m q) -> p m q", m=4)
                        else:
                            _, n, half = use
                            blocks = min(4, n // H + 1 - 4 * half)
                            if n >= 4:
                                act.wait_ge(s_pv, n // 2 - 1)
                            dst = dt_sb[:, 4 * half:4 * half + blocks, n % 4, :]
                            src = src[:, 0:blocks * P].rearrange("p (k q) -> p k q", q=P)
                        nc.scalar.activation(dst, src, ACT.Copy).then_inc(s_tfree, 1)

                    def double(t, chunk):
                        act.wait_ge(s_lo, g_index(t, chunk) + 1)
                        rows = hl[:, 16:24, :, :] if chunk == 2 else hl[:, 0:16, :, :]
                        src, dst = ((rows[:, :, 0:2, :], rows[:, :, 2:4, :]) if chunk == 2 else
                                    (rows[:, :, 0:4:2, :], rows[:, :, 1:4:2, :]))
                        nc.scalar.activation(dst, src, ACT.Copy).then_inc(s_hl, 1)

                    copy_out(T_FIRST[0])
                    double(0, 0)
                    for use in T_FIRST[1:3]:
                        copy_out(use)
                    double(0, 2)
                    for use in T_FIRST[3:]:
                        copy_out(use)
                    for n in range(STEPS):
                        duo = (n - 6) // 2
                        if n % 2 == 0 and 0 <= duo < DUOS:
                            act.wait_ge(s_pv, duo + 1)
                            if duo:
                                act.wait_ge(s_pvfree, duo)
                            nc.scalar.activation(r_sb[:, :], PV[:, P:2 * P], ACT.Copy).then_inc(s_rcopy, 1)
                        t, i = divmod(n, H)
                        if t < NT and i in TWICE_LATE:
                            double(t, TWICE_LATE[i])
                        if t + 1 < NT and i in TWICE_STEP:
                            double(t + 1, TWICE_STEP[i])
                        for m in range(2):
                            for use in t_uses(n, m):
                                copy_out(use)
                            if n >= NH:
                                continue
                            parts, w = halves(n // H)
                            act.wait_ge(s_negmax, 2 * n + m + 1)
                            if m == 0 and n >= 3:
                                act.wait_ge(s_tfull, T_INDEX["d", n - 3, (n - 3) // H // 4] + 1)
                            if n >= 2:
                                act.wait_ge(s_comb, n - 1)
                            e = (e1[n % 3], e2[n % 2])[m]
                            nc.scalar.activation(e[:, 0:parts * w].rearrange("p (h w) -> p h w", h=parts),
                                                 score_slot(n, m)[0], ACT.Exp,
                                                 bias=nmax[:, (2 * n + m) % 8:(2 * n + m) % 8 + 1], scale=1.0,
                                                 accum_out=lsum[:, n % 2, m:m + 1]).then_inc(s_exp, 1)

                @block.gpsimd
                def _(pool):
                    def add(g, piece):
                        cols = slice(piece * ADD, (piece + 1) * ADD)
                        pool.wait_ge(s_gfree, g + 1)
                        nc.gpsimd.tensor_tensor(t1[:, cols], t1[:, cols], t2[:, cols], ALU.add).then_inc(s_rot, 1)

                    for g in range(3):
                        for piece in range(pieces(CHUNKS[g])):
                            add(g, piece)
                    for n in range(NH):
                        pool.wait_ge(s_linv, n + 1)
                        if n >= 2:
                            pool.wait_ge(s_comb, n - 1)
                        nc.gpsimd.tensor_scalar(coef[:, n % 2:n % 2 + 1], lsum[:, n % 2, 0:1], linv[:, n % 8, 1:2],
                                                neglam[:, :], ALU.mult, ALU.mult).then_inc(s_coef, 1)
                        for piece in range(2):
                            t, i = divmod(n + 1 - piece, H)
                            chunk, part = ROTATE_STEP.get(i, (0, None))
                            if t + 1 < NT and part == 0 and piece < pieces(chunk):
                                add(g_index(t + 1, chunk), piece)

                @block.vector
                def _(dve):
                    def rotate(t, chunk, part):
                        g = g_index(t, chunk)
                        maps = 8 if chunk == 2 else 16
                        at = 16 if chunk == 2 else 0
                        a, c = t1[:, 0:maps * DH], t2[:, 0:maps * DH]
                        rows = hl[:, at:at + maps, :, :]
                        hi, lo = rows[:, :, 0, :], rows[:, :, 1 if chunk == 2 else 2, :]
                        bank = g_bank(g)
                        whole = a.rearrange("p (m d) -> p m d", d=DH)
                        if part == 0:
                            f = 2 if chunk == 2 else 0
                            cos = rope_sb[:, t, f:f + 1, :].broadcast_to((P, maps, DH))
                            sin = rope_sb[:, t, f + 1:f + 2, :].rearrange("p o (i s) -> p o i s", s=2)\
                                .broadcast_to((P, maps, DH // 2, 2))
                            if g:
                                dve.wait_ge(s_lo, g)
                            dve.wait_ge(s_gfull, g + 1)
                            if chunk == 2:
                                nc.vector.tensor_copy(v_sb[:, t, :], bank[:, KC:2 * KC])
                            nc.vector.tensor_tensor(a.rearrange("p (m d) -> p m d", d=DH),
                                                    bank[:, 0:maps * DH].rearrange("p (m d) -> p m d", d=DH), cos, ALU.mult)
                            nc.vector.tensor_tensor(
                                c.rearrange("p (m i s) -> p m i s", i=DH // 2, s=2),
                                bank[:, 0:maps * DH].rearrange("p (m i s) -> p m i s", i=DH // 2, s=2)[:, :, :, ::-1],
                                sin, ALU.mult).then_inc(s_gfree, 1)
                        elif part == 1:
                            dve.wait_ge(s_rot, g // 3 * sum(map(pieces, CHUNKS)) +
                                        sum(map(pieces, CHUNKS[:g % 3 + 1])))
                            before = {0: ("q", t - 1, 7), 1: ("q", t, 3), 2: ("k", t - 1, 1)}[chunk]
                            if before in T_INDEX:
                                dve.wait_ge(s_tfull, T_INDEX[before] + 1)
                            nc.vector.tensor_scalar(hi.bitcast(I32), whole.bitcast(I32), HI_BITS, None,
                                                    ALU.bitwise_and).then_inc(s_hi, 1)
                        else:
                            dve.wait_ge(s_hi, g + 1)
                            nc.vector.tensor_tensor(lo, whole, hi, ALU.subtract).then_inc(s_lo, 1)

                    def neg_max(n, m):
                        u = 2 * n + m
                        dve.wait_ge(s_score, u + 1)
                        nc.vector.tensor_reduce(nmax[:, u % 8:u % 8 + 1], score_slot(n, m)[0], AX.XY, ALU.max,
                                                negate=True).then_inc(s_negmax, 1)

                    for chunk, part in ((0, 0), (0, 1), (0, 2), (2, 0), (2, 1), (2, 2), (1, 0)):
                        rotate(0, chunk, part)
                    for step in range(STEPS):
                        n = step - 1
                        duo = (step - 6) // 2
                        done = step % 2 == 0 and 0 <= duo < DUOS
                        if step < NH:
                            neg_max(step, 0)
                        if done:
                            t, i = divmod(2 * duo, H)
                            pair, _, j = head_of(i)
                            dve.wait_ge(s_rcopy, duo + 1)
                            nc.vector.tensor_tensor(attn_t[:, pair, j, t * P:(t + 1) * P], PV[:, 0:P], r_sb[:, :],
                                                    ALU.mult).then_inc(s_pvfree, 1)
                        if 0 <= n < NH:
                            dve.wait_ge(s_exp, 2 * n + 2)
                            nc.vector.reciprocal(linv[:, n % 8, :], lsum[:, n % 2, :]).then_inc(s_linv, 1)
                        if step < NH:
                            neg_max(step, 1)
                        if 0 <= n < NH:
                            w = (n // H + 1) * P
                            dve.wait_ge(s_coef, n + 1)
                            nc.vector.scalar_tensor_tensor(e1[n % 3][:, 0:w], e2[n % 2][:, 0:w],
                                                           coef[:, n % 2:n % 2 + 1], e1[n % 3][:, 0:w],
                                                           ALU.mult, ALU.add).then_inc(s_comb, 1)
                        t, i = divmod(step, H)
                        if t < NT and i in ROTATE_LATE:
                            rotate(t, *ROTATE_LATE[i])
                        if t + 1 < NT and i in ROTATE_STEP:
                            rotate(t + 1, *ROTATE_STEP[i])
                        if t == 4 and 6 <= i < 14:
                            if i == 6:
                                dve.wait_ge(s_pvfree, DUOS // 2)
                            j = i - 6
                            nc.vector.bn_stats(gstat[:, j, 0, :], attn_t[:, j // 4, j % 4, 0:T // 2])
                        if NH <= step < NH + 4:
                            if step == NH:
                                dve.wait_ge(s_pvfree, DUOS - 8)
                            for j in range(2 * (step - NH), 2 * (step - NH) + 2):
                                nc.vector.bn_stats(gstat[:, j, 1, :], attn_t[:, j // 4, j % 4, T // 2:T - P])

            with ExitStack() as mix:
                x1 = sb("x1", [P, NT, D], scope=mix)
                x1_hi = sb("x1_hi", [P, DC, T], F16, mix)
                x1_lo = sb("x1_lo", [P, DC, T], F16, mix)
                hid_hi = sb("hid_hi", [P, EB, BANK], F16, mix)
                hid_lo = sb("hid_lo", [P, EB, BANK], F16, mix)
                sl = sb("sl", [P, 2, BANK], scope=mix)
                hh = sb("hh", [P, 2, BANK], scope=mix)
                mv = sb("mv", [P, 8, 2], scope=mix)
                gm = sb("gm", [P, 8], scope=mix)
                dm = sb("dm", [P, 8], scope=mix)
                rv = sb("rv", [P, 8], scope=mix)
                gv = sb("gv", [P, 8], scope=mix)
                rs = sb("rs", [P, 8], scope=mix)
                fac = sb("fac", [P, 8], scope=mix)
                off = sb("off", [P, 8], scope=mix)
                lst = sb("lst", [P, 2, 6], scope=mix)
                lmv = sb("lmv", [P, 2, 2], scope=mix)
                lrs = sb("lrs", [P, 2], scope=mix)
                block = mix.enter_context(nc.Block())
                Y = [PV, G]
                NF = 2 * EB
                NORM = ((0, P), (P, T // 2), (T // 2, T))
                NY = 2 * NT

                @block.sync
                def _(sp):
                    for k in range(4):
                        sp.dma_start(x1[:, 2 * k:2 * k + 2, :],
                                     x_tiles[bass.ds(b * NT + 2 * k, 2)].rearrange("t p d -> p t d"))\
                            .then_inc(s_xr[k], 16)
                    for k in range(2):
                        load_x(sp, b * NT + NT + k, k)
                    for s in att_sems:
                        sp.sem_clear(s)
                    sp.wait_ge(s_y, NT)
                    load_qkv(sp, s_qkv2)
                    for k in range(NT):
                        sp.wait_ge(s_ready, k + 1)
                        sp.dma_start(out_tiles[bass.ds(b, 1), k].rearrange("o p d -> p (o d)"), z[:, k % 2, :])\
                            .then_inc(s_od[k % 2], 16)
                    sp.wait_ge(s_qkv2, N_QKV)

                @block.gpsimd
                def _(pool):
                    pool.wait_ge(s_gr, 1)
                    nc.gpsimd.tensor_scalar(gv[:, :], gv[:, :], LN_EPS, None, ALU.add).then_inc(s_eps, 1)
                    pool.wait_ge(s_eps, 1)
                    nc.gpsimd.tensor_tensor(rs[:, :], gv[:, :], mhalf[:, :], ALU.pow).then_inc(s_grs, 1)
                    for k in range(NY):
                        pool.wait_ge(s_var, k + 1)
                        veps = lmv[:, k % 2, 1:2]
                        nc.gpsimd.tensor_scalar(veps, veps, LN_EPS, None, ALU.add).then_inc(s_eps, 1)
                        pool.wait_ge(s_eps, k + 2)
                        nc.gpsimd.tensor_tensor(lrs[:, k % 2:k % 2 + 1], veps, mhalf[:, 0:1], ALU.pow)\
                            .then_inc(s_rstd, 1)

                @block.tensor
                def _(pe):
                    def x1_transposed(k):
                        pe.wait_ge(s_x1, k + 1)
                        if k >= 2:
                            pe.wait_ge(s_xlo, k - 1)
                        for c in range(DC):
                            last = nc.tensor.transpose(TB[k % 2][:, c * P:(c + 1) * P], x1[:, k, c * P:(c + 1) * P],
                                                       ident[:, :])
                        last.then_inc(s_x1T, 1)

                    def up_gate(f):
                        ch, eb = divmod(f, EB)
                        if f == 0:
                            pe.wait_ge(s_xlo, 4)
                        if f == EB:
                            pe.wait_ge(s_xlo, 8)
                        if f >= 2:
                            pe.wait_ge(s_h, f - 1)
                        for k, w in enumerate((up_t, gate_t)):
                            for c in range(DC):
                                for part in (x1_hi, x1_lo):
                                    last = nc.tensor.matmul(S[f % 2][:, k, :], w[:, c, eb * P:(eb + 1) * P],
                                                            part[:, c, ch * BANK:(ch + 1) * BANK],
                                                            start=c == 0 and part is x1_hi,
                                                            stop=c == DC - 1 and part is x1_lo)
                        last.then_inc(s_ug, 1)

                    pe.wait_ge(s_mv, 1)
                    nc.tensor.matmul(TB[0][:, 0:8], blk64[:, :], mv[:, :, 0], start=True, stop=True).then_inc(s_gm, 1)
                    pe.wait_ge(s_gv, 1)
                    nc.tensor.matmul(TB[1][:, 0:8], blk64[:, :], rv[:, :], start=True, stop=True).then_inc(s_gvm, 1)
                    for k in range(NT):
                        part = [a <= k * P < e for a, e in NORM].index(True)
                        pe.wait_ge(s_nv, 4 * part + 4)
                        pe.wait_ge(s_na, 4 * part + 4)
                        if k >= 2:
                            pe.wait_ge(s_yfree, k - 1)
                        for c in range(8):
                            last = nc.tensor.matmul(Y[k % 2][:, :], attn_t[:, c // 4, c % 4, k * P:(k + 1) * P],
                                                    wo_sb[:, c, :], start=c == 0, stop=c == 7)
                        last.then_inc(s_y, 1)
                        if k >= 2:
                            x1_transposed(k - 2)
                    up_gate(0)
                    x1_transposed(NT - 2)
                    x1_transposed(NT - 1)
                    for ch in range(2):
                        for eb in range(EB):
                            if ch or eb:
                                up_gate(ch * EB + eb)
                        for j in range(4):
                            y = NT + 4 * ch + j
                            pe.wait_ge(s_yfree, y - 1)
                            for eb in range(EB):
                                if j == 0:
                                    pe.wait_ge(s_hlo, ch * EB + eb + 1)
                                for part in (hid_hi, hid_lo):
                                    last = nc.tensor.matmul(Y[y % 2][:, :], part[:, eb, j * P:(j + 1) * P],
                                                            down_t[:, eb, :], start=eb == 0 and part is hid_hi,
                                                            stop=eb == EB - 1 and part is hid_lo)
                            last.then_inc(s_y, 1)

                @block.scalar
                def _(act):
                    def x1_high(k):
                        act.wait_ge(s_x1T, k + 1)
                        nc.scalar.activation(x1_hi[:, :, k * P:(k + 1) * P],
                                             TB[k % 2][:, :].rearrange("p (c q) -> p c q", c=DC),
                                             ACT.Copy, scale=XS).then_inc(s_xhi, 1)

                    def hidden_high(f):
                        act.wait_ge(s_h, f + 1)
                        if f >= EB and f % EB == 0:
                            act.wait_ge(s_y, NT + 4 * (f // EB))
                        nc.scalar.activation(hid_hi[:, f % EB, :], hh[:, f % 2, :], ACT.Copy).then_inc(s_hhi, 1)

                    act.wait_ge(s_aff, 1)
                    for a, e in NORM:
                        for j in range(4, 8):
                            v = attn_t[:, j // 4, j % 4, a:e]
                            nc.scalar.activation(v, v, ACT.Identity, bias=off[:, j:j + 1], scale=fac[:, j:j + 1])\
                                .then_inc(s_na, 1)
                    for k in range(NT - 2):
                        x1_high(k)
                    for f in range(NF):
                        act.wait_ge(s_ug, f + 1)
                        if f >= 2:
                            act.wait_ge(s_h, f - 1)
                        nc.scalar.activation(sl[:, f % 2, :], S[f % 2][:, 0, :], ACT.Silu, scale=k_silu[:, :])\
                            .then_inc(s_sl, 1)
                        if f == 0:
                            x1_high(NT - 2)
                            x1_high(NT - 1)
                        if f % EB:
                            hidden_high(f - 1)
                        if f % EB == EB - 1:
                            hidden_high(f)

                @block.vector
                def _(dve):
                    chain = [0]

                    def link(ins):
                        chain[0] += 1
                        ins.then_inc(s_dve2, 1)
                        dve.wait_ge(s_dve2, chain[0])

                    def variance(k, v):
                        link(nc.vector.bn_stats(lst[:, k % 2, :], v))
                        nc.vector.bn_aggr(lmv[:, k % 2, :], lst[:, k % 2, :]).then_inc(s_var, 1)

                    def normalised(k, v):
                        dve.wait_ge(s_rstd, k + 1)
                        return nc.vector.tensor_scalar(v, v, lmv[:, k % 2, 0:1], lrs[:, k % 2:k % 2 + 1],
                                                       ALU.subtract, ALU.mult)

                    def x1_low(k):
                        dve.wait_ge(s_xhi, k + 1)
                        nc.vector.scalar_tensor_tensor(x1_lo[:, :, k * P:(k + 1) * P],
                                                       TB[k % 2][:, :].rearrange("p (c q) -> p c q", c=DC), XS,
                                                       x1_hi[:, :, k * P:(k + 1) * P], ALU.mult, ALU.subtract)\
                            .then_inc(s_xlo, 1)

                    def hidden_low(f):
                        dve.wait_ge(s_hhi, f + 1)
                        nc.vector.tensor_tensor(hid_lo[:, f % EB, :], hh[:, f % 2, :], hid_hi[:, f % EB, :],
                                                ALU.subtract).then_inc(s_hlo, 1)

                    for j in range(8):
                        last = nc.vector.bn_stats(gstat[:, j, 2, :], attn_t[:, j // 4, j % 4, T - P:T])
                    last.then_inc(s_gst, 1)
                    dve.wait_ge(s_gst, 1)
                    for j in range(8):
                        last = nc.vector.bn_aggr(mv[:, j, :], gstat[:, j, :, :].rearrange("p h s -> p (h s)"))
                    last.then_inc(s_mv, 1)
                    dve.wait_ge(s_gm, 1)
                    nc.vector.tensor_copy(gm[:, :], TB[0][:, 0:8])
                    dve.wait_ge(s_mv, 1)
                    link(nc.vector.tensor_tensor(dm[:, :], mv[:, :, 0], TB[0][:, 0:8], ALU.subtract))
                    link(nc.vector.tensor_tensor(dm[:, :], dm[:, :], dm[:, :], ALU.mult))
                    nc.vector.tensor_tensor(rv[:, :], dm[:, :], mv[:, :, 1], ALU.add).then_inc(s_gv, 1)
                    dve.wait_ge(s_gvm, 1)
                    nc.vector.tensor_copy(gv[:, :], TB[1][:, 0:8]).then_inc(s_gr, 1)
                    dve.wait_ge(s_grs, 1)
                    link(nc.vector.tensor_tensor(fac[:, :], gn_sb[:, 0, :], rs[:, :], ALU.mult))
                    link(nc.vector.tensor_scalar(fac[:, :], fac[:, :], 1.0 - LAMBDA_INIT, None, ALU.mult))
                    link(nc.vector.tensor_tensor(dm[:, :], gm[:, :], fac[:, :], ALU.mult))
                    nc.vector.scalar_tensor_tensor(off[:, :], gn_sb[:, 1, :], 1.0 - LAMBDA_INIT, dm[:, :],
                                                   ALU.mult, ALU.subtract).then_inc(s_aff, 1)
                    dve.wait_ge(s_aff, 1)
                    for a, e in NORM:
                        for j in range(4):
                            v = attn_t[:, j // 4, j % 4, a:e]
                            nc.vector.tensor_scalar(v, v, fac[:, j:j + 1], off[:, j:j + 1], ALU.mult, ALU.add)\
                                .then_inc(s_nv, 1)

                    for k in range(NT + 1):
                        if k < NT:
                            dve.wait_ge(s_xr[k // 2], 16)
                            dve.wait_ge(s_y, k + 1)
                            nc.vector.tensor_tensor(x1[:, k, :], Y[k % 2][:, :], x1[:, k, :], ALU.add)\
                                .then_inc(s_yfree, 1)
                            dve.wait_ge(s_yfree, k + 1)
                            variance(k, x1[:, k, :])
                        if k >= 1:
                            normalised(k - 1, x1[:, k - 1, :]).then_inc(s_x1, 1)
                        if k >= 3:
                            x1_low(k - 3)

                    for ch in range(2):
                        for eb in range(EB):
                            f = ch * EB + eb
                            dve.wait_ge(s_sl, f + 1)
                            if f >= 2:
                                dve.wait_ge(s_hhi, f - 1)
                                dve.wait_ge(s_hlo, f - 1)
                            nc.vector.scalar_tensor_tensor(hh[:, f % 2, :], sl[:, f % 2, :], k_hid[:, :],
                                                           S[f % 2][:, 1, :], ALU.mult, ALU.mult).then_inc(s_h, 1)
                            if f == 0:
                                x1_low(NT - 2)
                                x1_low(NT - 1)
                            if eb:
                                hidden_low(f - 1)
                        hidden_low(ch * EB + EB - 1)
                        for j in range(4):
                            k = 4 * ch + j
                            y = NT + k
                            v = z[:, k % 2, :]
                            dve.wait_ge(s_y, y + 1)
                            dve.wait_ge(s_od[k % 2], b * ROUND_IO + 16 * (k // 2) + 1)
                            nc.vector.scalar_tensor_tensor(v, Y[y % 2][:, :], k_out[:, :], x1[:, k, :],
                                                           ALU.mult, ALU.add).then_inc(s_yfree, 1)
                            dve.wait_ge(s_yfree, y + 1)
                            variance(y, v)
                            normalised(y, v).then_inc(s_ready, 1)

        with nc.Block() as block:
            @block.sync
            def _(sp):
                for k in range(2):
                    sp.wait_ge(s_od[k], B * ROUND_IO + 1)
                    sp.wait_ge(s_xin[k], B * ROUND_IO + 16)


def rope_table():
    inv = (1.0 / np.float32(10000.0) ** (np.arange(0, DH, 2, dtype=np.float32) / np.float32(DH))).astype(np.float32)
    freqs = np.arange(T, dtype=np.float32)[:, None] * inv[None, :]
    cos = np.repeat(np.cos(freqs), 2, axis=1)
    sin = np.repeat(np.sin(freqs), 2, axis=1) * np.tile(np.array([-1.0, 1.0], np.float32), DH // 2)
    s = np.float32(1.0 / math.sqrt(DH))
    return np.ascontiguousarray(np.stack([cos * s, sin * s, cos, sin], axis=1).astype(np.float32))


def kernel(**inputs):
    import concourse.bacc as bacc
    from concourse.bass_utils import run_bass_kernel_spmd

    nc = bacc.Bacc("TRN2", target_bir_lowering=False, num_devices=1)
    a = {n.removeprefix("L0_attn_"): np.asarray(v) for n, v in inputs.items()}
    wq = a["Wq"].reshape(D, 2, 2, 4, 2 * DH).transpose(0, 1, 3, 2, 4).reshape(D, QC)
    by_row = lambda v: v.reshape(2, 2, 4, 2 * DH, -1).transpose(0, 2, 1, 3, 4).reshape(8 * P, -1)
    gn = np.stack([by_row(a[n]).reshape(8, P).T for n in ("gn_w", "gn_b")], axis=1)
    arrays = {
        "in_x": np.concatenate([a["x"].reshape(B * T, D), a["x"].reshape(B * T, D)[:2 * P]]), "in_w_qkv": np.concatenate([wq, a["Wk"], a["Wv"]], axis=1), "in_wo": by_row(a["Wo"]),
        "in_lambda": np.stack([a["lambda_q1"], a["lambda_k1"], a["lambda_q2"], a["lambda_k2"]]).reshape(2, 2, DH),
        "in_gn": gn, "in_w_up": a["L0_ffn_W_up"].T, "in_w_gate": a["L0_ffn_W_gate"].T, "in_w_down": a["L0_ffn_W_down"].T,
        "in_rope": rope_table(),
    }
    arrays = {n: np.ascontiguousarray(v) for n, v in arrays.items()}
    args = [nc.dram_tensor(n, a.shape, mybir.dt.from_np(a.dtype), kind="ExternalInput").ap() for n, a in arrays.items()]
    args.append(nc.dram_tensor("out", (B, T, D), F32, kind="ExternalOutput").ap())
    layer_kernel(nc, *args)
    r = run_bass_kernel_spmd(nc, [arrays], core_ids=[0])
    return r.results[0]["out"]
```
